# Optimizing a Trainium2 kernel written in Bass

```python
import numpy as np
import jax
import jax.numpy as jnp

def _softmax(x, axis=-1):
    return jax.nn.softmax(x, axis=axis)

def _gelu(x):
    return jax.nn.gelu(x, approximate=True)

def _silu(x):
    return jax.nn.silu(x)

def _sigmoid(x):
    return jax.nn.sigmoid(x)

def _layernorm(x, axis=-1, eps=1e-05):
    m = jnp.mean(x, axis=axis, keepdims=True)
    v = jnp.var(x, axis=axis, keepdims=True)
    return (x - m) / jnp.sqrt(v + eps)

def _scatter_add(tgt, idx, src, axis=0):
    return tgt.at[idx].add(src)

def _segment_sum(src, seg, n):
    return jax.ops.segment_sum(src, seg, n)
kernel_name = 'mk_xattn_seq_d1_seqx_r4_54599c'

def setup_inputs(seed: int=0):
    np.random.seed(seed)
    _w = jnp.asarray

    def _rec_inputs():
        import jax
        import jax.numpy as jnp
        _rk = jax.random.key(seed)
        x = -0.0001548 + 1 * jax.random.normal(jax.random.fold_in(_rk, 1), (32, 128, 320), jnp.float32)
        _lenS = 128 - jax.random.randint(jax.random.fold_in(_rk, 7), (32,), 0, max(1, 128 // 4) + 1, jnp.int32)
        _lenS2 = 128 - jax.random.randint(jax.random.fold_in(_rk, 8), (32,), 0, max(1, 128 // 4) + 1, jnp.int32)
        _ctx_768P = jax.random.normal(jax.random.fold_in(_rk, 11), (32, 16, 192), jnp.float32)
        _ctx_768c = jax.random.dirichlet(jax.random.fold_in(_rk, 511), 0.3 * jnp.ones((16,), jnp.float32), (32, 128))
        _ctx_768t = jnp.einsum('bsk,bkd->bsd', _ctx_768c, _ctx_768P)
        _ctx_768t = _ctx_768t * jax.lax.rsqrt(jnp.mean(jnp.square(_ctx_768t)) + 1e-12) * 0.953939
        ctx_768 = 0.00141353 + 0.998943 * (_ctx_768t + 0.3 * jax.random.normal(jax.random.fold_in(_rk, 611), (32, 128, 192), jnp.float32))
        return (x, ctx_768)
    x, ctx_768 = _rec_inputs()

    def _L0_xattn_setup():
        import jax, jax.numpy as jnp
        import numpy as np
        HEADS = 8
        NUM_TOKENS = 4
        CROSS_ATTENTION_DIM = 192

        def _mha(q, k, v, heads=HEADS):
            B, Sq, H = q.shape
            Sk = k.shape[1]
            d = H // heads
            qh = q.reshape(B, Sq, heads, d).transpose(0, 2, 1, 3)
            kh = k.reshape(B, Sk, heads, d).transpose(0, 2, 1, 3)
            vh = v.reshape(B, Sk, heads, d).transpose(0, 2, 1, 3)
            scores = jnp.einsum('bhqd,bhkd->bhqk', qh, kh) * jnp.asarray(d, q.dtype) ** (-0.5)
            probs = jax.nn.softmax(scores, axis=-1)
            out = jnp.einsum('bhqk,bhkd->bhqd', probs, vh)
            return out.transpose(0, 2, 1, 3).reshape(B, Sq, H)
        key = jax.random.key(seed)
        ks = jax.random.split(key, 10)
        B, S, H, CAD, T = (4, 256, 320, CROSS_ATTENTION_DIM, NUM_TOKENS)
        sc = 0.02
        return {'hidden_states': jax.random.normal(ks[0], (B, S, H), jnp.float32), 'encoder_hidden_states': jax.random.normal(ks[1], (B, 77 + T, CAD), jnp.float32), 'Wq': jax.random.normal(ks[2], (H, H), jnp.float32) * sc, 'Wk': jax.random.normal(ks[3], (CAD, H), jnp.float32) * sc, 'Wv': jax.random.normal(ks[4], (CAD, H), jnp.float32) * sc, 'Wq_ca': jax.random.normal(ks[5], (T, H), jnp.float32) * sc, 'Wk_ca': jax.random.normal(ks[6], (CAD, H), jnp.float32) * sc, 'Wv_ca': jax.random.normal(ks[7], (CAD, H), jnp.float32) * sc, 'Wout': jax.random.normal(ks[8], (H, H), jnp.float32) * sc, 'b_out': jnp.zeros((H,), jnp.float32)}
    _L0_xattn_all = _L0_xattn_setup()
    _L0_xattn_in = {k: v for k, v in _L0_xattn_all.items() if k in ('Wq', 'Wk', 'Wv', 'Wq_ca', 'Wk_ca', 'Wv_ca', 'Wout', 'b_out')}
    del _L0_xattn_all
    return {'x': x, 'ctx_768': ctx_768, 'L0_xattn_Wq': _L0_xattn_in['Wq'], 'L0_xattn_Wk': _L0_xattn_in['Wk'], 'L0_xattn_Wv': _L0_xattn_in['Wv'], 'L0_xattn_Wq_ca': _L0_xattn_in['Wq_ca'], 'L0_xattn_Wk_ca': _L0_xattn_in['Wk_ca'], 'L0_xattn_Wv_ca': _L0_xattn_in['Wv_ca'], 'L0_xattn_Wout': _L0_xattn_in['Wout'], 'L0_xattn_b_out': _L0_xattn_in['b_out']}

def reference(x, ctx_768, L0_xattn_Wq, L0_xattn_Wk, L0_xattn_Wv, L0_xattn_Wq_ca, L0_xattn_Wk_ca, L0_xattn_Wv_ca, L0_xattn_Wout, L0_xattn_b_out):
    import jax
    import jax.numpy as jnp

    def _L0_xattn_ref(hidden_states, encoder_hidden_states, Wq, Wk, Wv, Wq_ca, Wk_ca, Wv_ca, Wout, b_out):
        import jax, jax.numpy as jnp
        import numpy as np
        HEADS = 8
        NUM_TOKENS = 4
        CROSS_ATTENTION_DIM = 192

        def _mha(q, k, v, heads=HEADS):
            B, Sq, H = q.shape
            Sk = k.shape[1]
            d = H // heads
            qh = q.reshape(B, Sq, heads, d).transpose(0, 2, 1, 3)
            kh = k.reshape(B, Sk, heads, d).transpose(0, 2, 1, 3)
            vh = v.reshape(B, Sk, heads, d).transpose(0, 2, 1, 3)
            scores = jnp.einsum('bhqd,bhkd->bhqk', qh, kh) * jnp.asarray(d, q.dtype) ** (-0.5)
            probs = jax.nn.softmax(scores, axis=-1)
            out = jnp.einsum('bhqk,bhkd->bhqd', probs, vh)
            return out.transpose(0, 2, 1, 3).reshape(B, Sq, H)
        residual = hidden_states
        unet_size = residual.shape[1]
        end_pos = encoder_hidden_states.shape[1] - NUM_TOKENS
        enc = encoder_hidden_states[:, :end_pos, :]
        ca = encoder_hidden_states[:, end_pos:, :]
        query = hidden_states @ Wq
        keyt = enc @ Wk
        valt = enc @ Wv
        hs = _mha(query, keyt, valt)
        ca_q1 = jnp.einsum('btc,th->bch', ca, Wq_ca)
        indices = np.linspace(0, CROSS_ATTENTION_DIM - 1, unet_size).astype(np.int64)
        ca_q1 = ca_q1[:, indices, :]
        ca_hs1 = _mha(ca_q1, residual, residual)
        ca_q2 = ca_hs1 @ Wq
        ca_k2 = ca @ Wk_ca
        ca_v2 = ca @ Wv_ca
        ca_hs2 = _mha(ca_q2, ca_k2, ca_v2)
        out = hs + ca_hs2
        out = out @ Wout + b_out
        out = out + residual
        return out
    x = _L0_xattn_ref(x, ctx_768, L0_xattn_Wq, L0_xattn_Wk, L0_xattn_Wv, L0_xattn_Wq_ca, L0_xattn_Wk_ca, L0_xattn_Wv_ca, L0_xattn_Wout, L0_xattn_b_out)
    return x

_drawn_inputs = setup_inputs


def setup_inputs(seed=0):
    import zlib

    import numpy as np

    out = dict(_drawn_inputs(seed))
    spreads = {'L0_xattn_b_out': (0.0, 0.1)}
    factors = {'L0_xattn_Wq': 8.0, 'L0_xattn_Wk': 8.0, 'L0_xattn_Wq_ca': 35.682, 'L0_xattn_Wk_ca': 8.0}
    for name, (base, spread) in spreads.items():
        noise = np.random.default_rng([zlib.crc32(name.encode()), seed]).standard_normal(out[name].shape)
        drawn = base * np.exp(spread * noise) if base else spread * noise
        out[name] = jnp.asarray(drawn.astype(out[name].dtype))
    for name, factor in factors.items():
        out[name] = (out[name] * factor).astype(out[name].dtype)
    return out
```

```python
import concourse.bass as bass
from concourse import mybir
from contextlib import ExitStack

B, S, H, CAD, T, HEADS = 32, 128, 320, 192, 4, 8
D = H // HEADS
SE = S - T
NC = 4
SLOT = 64
NM = 6
XR, NX = 120, 3
X_AT = (0, XR, H - XR)
CR, NK = 96, 2
SCALE = float(D) ** -0.5
UNITS = 4


class Memory:
    pass


def tensors(nc, ctx):
    f32, bf16 = mybir.dt.float32, mybir.dt.bfloat16

    m = Memory()

    def sb(name, shape, dt=f32):
        return ctx.enter_context(nc.sbuf_tensor(name, shape, dt))

    m.wq = sb("wq", [XR, NX, NC, 128])
    m.wqs = sb("wqs", [XR, NX, NC, 128])
    m.wk = sb("wk", [CR, NK, NC, 128])
    m.wv = sb("wv", [CR, NK, H])
    m.wkca = sb("wkca", [CR, NK, NC, 128])
    m.wvca = sb("wvca", [CR, NK, H])
    m.wout = sb("wout", [XR, NX, H])
    m.bias = sb("bias", [128, H])
    m.signs = sb("signs", [128, 4])
    m.ident = sb("ident", [128, 128])
    m.ca_raw = sb("ca_raw", [128, B, CAD])
    m.ca_nat = sb("ca_nat", [128, CAD])
    m.caT = sb("caT", [CR, NK, 128])
    m.wqT = sb("wqT", [128, NX, NC, XR])
    m.k2T = sb("k2T", [128, NC, 128])
    m.g = sb("g", [XR, NX, B, HEADS * T])
    m.v2 = sb("v2", [128, H])
    m.v2blk = sb("v2blk", [HEADS * T, B, H])
    m.x = sb("x", [128, 2, H])
    m.c = sb("c", [128, 2, CAD])
    m.xe = sb("xe", [128, 2, HEADS, D + 1])
    m.xb = sb("xb", [128, 2, H])
    m.xT = sb("xT", [XR, NX, 128])
    m.cT = sb("cT", [CR, NK, 128])
    m.kT = sb("kT", [128, NC, SE])
    m.qT = sb("qT", [128, NC, 128])
    m.v = sb("v", [SE, 2, HEADS, D + 1])
    m.m_hi = sb("m_hi", [128, NC, 128], bf16)
    m.m_res = sb("m_res", [128, NC, 128])
    m.m_mid = sb("m_mid", [128, NC, 128], bf16)
    m.m_st = sb("m_st", [128, NC, 128], bf16)
    m.c_gath = sb("c_gath", [128, 128])
    m.zero = sb("zero", [128, 1])
    m.c_hi = sb("c_hi", [128, 128], bf16)
    m.c_tmp = sb("c_tmp", [128, 128])
    m.c_res = sb("c_res", [128, 128])
    m.c_mid = sb("c_mid", [128, 128], bf16)
    m.c_tmp2 = sb("c_tmp2", [128, 128])
    m.c_st = sb("c_st", [128, 2, 128], bf16)
    m.smax = sb("smax", [128, 2, NC])
    m.shift = sb("shift", [128, 2, NC, 128])
    m.p = sb("p", [128, NC, 128])
    m.rec = sb("rec", [128, 2, NC])
    m.hs = sb("hs", [128, 2, H])
    m.ca = sb("ca", [128, H])
    m.aT = sb("aT", [XR, NX, 128])
    m.max3 = sb("max3", [128, HEADS])
    m.sh3 = sb("sh3", [128, HEADS * T])
    m.p3 = sb("p3", [128, HEADS * T])
    m.sum3 = sb("sum3", [128, HEADS])
    m.rec3 = sb("rec3", [128, HEADS])
    m.p3n = sb("p3n", [128, HEADS * T])
    m.p3T = sb("p3T", [HEADS * T, 128])
    m.osum = sb("osum", [128, H])
    m.oT = sb("oT", [XR, NX, 128])
    m.y = sb("y", [128, 2, H])
    def bank(name):
        return ctx.enter_context(nc.psum_tensor(name, [128, 512], f32))

    m.s_bank = [bank("s_bank0"), bank("s_bank1")]
    m.st_bank = bank("st_bank")
    m.pv_bank = bank("pv_bank")
    m.ring = [bank(f"ring{r}") for r in range(4)]
    return m


class Semaphores:
    pass


def semaphores(nc, ctx):
    def sem(name):
        return ctx.enter_context(nc.semaphore(name))

    s = Semaphores()
    s.x_loaded0 = sem("x_loaded0")
    s.x_loaded1 = sem("x_loaded1")
    s.c_loaded0 = sem("c_loaded0")
    s.c_loaded1 = sem("c_loaded1")
    s.wq_loaded = sem("wq_loaded")
    s.wk_loaded = sem("wk_loaded")
    s.wv_loaded = sem("wv_loaded")
    s.wout_loaded = sem("wout_loaded")
    s.small_loaded = sem("small_loaded")
    s.ca_loaded = sem("ca_loaded")
    s.ca_nat_loaded = sem("ca_nat_loaded")
    s.wca_loaded = sem("wca_loaded")
    s.ident_zeroed = sem("ident_zeroed")
    s.ident_made = sem("ident_made")
    s.zero_made = sem("zero_made")
    s.ca_zeroed = sem("ca_zeroed")
    s.v2_zeroed = sem("v2_zeroed")
    s.v2_placed = sem("v2_placed")
    s.ones_v = sem("ones_v")
    s.ones_x = sem("ones_x")
    s.wq_scaled = sem("wq_scaled")
    s.ca_fixed = sem("ca_fixed")
    s.setup_made = sem("setup_made")
    s.setup_copied = sem("setup_copied")
    s.xT_made = sem("xT_made")
    s.cT_made = sem("cT_made")
    s.kT_made = sem("kT_made")
    s.v_made = sem("v_made")
    s.qT_made = sem("qT_made")
    s.s_made = sem("s_made")
    s.st_made = sem("st_made")
    s.pv_made = sem("pv_made")
    s.aT_made = sem("aT_made")
    s.s3_made = sem("s3_made")
    s.p3T_made = sem("p3T_made")
    s.o3_made = sem("o3_made")
    s.oT_made = sem("oT_made")
    s.y_made = sem("y_made")
    s.xT_copied = sem("xT_copied")
    s.cT_copied = sem("cT_copied")
    s.kT_copied = sem("kT_copied")
    s.v_copied = sem("v_copied")
    s.qT_copied = sem("qT_copied")
    s.m_hi_made = sem("m_hi_made")
    s.m_res_made = sem("m_res_made")
    s.m_mid_made = sem("m_mid_made")
    s.m_stacked = sem("m_stacked")
    s.c_step = sem("c_step")
    s.c_stacked = sem("c_stacked")
    s.xe_copied = sem("xe_copied")
    s.xb_made = sem("xb_made")
    s.maxed = sem("maxed")
    s.shifted = sem("shifted")
    s.exped = sem("exped")
    s.reced = sem("reced")
    s.normed = sem("normed")
    s.aT_copied = sem("aT_copied")
    s.max3_made = sem("max3_made")
    s.sh3_made = sem("sh3_made")
    s.p3_made = sem("p3_made")
    s.sum3_made = sem("sum3_made")
    s.rec3_made = sem("rec3_made")
    s.p3n_made = sem("p3n_made")
    s.p3T_copied = sem("p3T_copied")
    s.o_summed = sem("o_summed")
    s.oT_copied = sem("oT_copied")
    s.y_added = sem("y_added")
    s.stored0 = sem("stored0")
    s.stored1 = sem("stored1")
    return s


def wait(eng, sem, count):
    if not isinstance(count, int) or count > 0:
        eng.wait_ge(sem, count)


def run_batches(eng, step):
    step(0, -1, True, False, False)
    step(0, 0, True, True, False)
    step(0, 1, True, True, True)
    with eng.Fori(1, B // 2 - 1) as i:
        step(i, 0, True, True, True)
        step(i, 1, True, True, True)
    last = B // 2 - 1
    step(last, 0, True, True, True)
    step(last, 1, False, True, True)
    step(last, 2, False, False, True)


def xattn_kernel(nc, x, c, wq_pad, wk_pad, wkca_pad, wv, wvca, wout, bias, signs, out):
    ACT, ALU, AX = mybir.ActivationFunctionType, mybir.AluOpType, mybir.AxisListType
    ctx = ExitStack()
    with ctx:
        m = tensors(nc, ctx)
        s = semaphores(nc, ctx)
        x_loaded, c_loaded = (s.x_loaded0, s.x_loaded1), (s.c_loaded0, s.c_loaded1)
        stored = (s.stored0, s.stored1)
        block = ctx.enter_context(nc.Block())

        def heads_of(t, slot):
            return t.rearrange("p (c j d) -> p c j d", c=NC, j=2)[:, :, slot, :]

        @block.sync
        def _(sp):
            def load(i, u):
                sp.dma_start(m.x[:, u % 2, :], x[bass.ds(2 * i + u, 1)].rearrange("b s h -> (b s) h")
                             ).then_inc(x_loaded[u % 2], 16)
                sp.dma_start(m.c[:, u % 2, :], c[bass.ds(2 * i + u, 1)].rearrange("b s h -> (b s) h")
                             ).then_inc(c_loaded[u % 2], 16)

            load(0, 0)
            sp.dma_start(m.wk[:, :, :, :], wk_pad).then_inc(s.wk_loaded, 16)
            sp.dma_start(m.wv[:, :, :], wv).then_inc(s.wv_loaded, 16)
            load(0, 1)
            sp.dma_start(m.bias[:, :], bias).then_inc(s.small_loaded, 16)
            sp.dma_start(m.ca_nat[:, :], c[:, SE:S, :]).then_inc(s.ca_nat_loaded, 16)
            sp.dma_start(m.wkca[:, :, :, :], wkca_pad).then_inc(s.wca_loaded, 16)
            sp.dma_start(m.wvca[:, :, :], wvca).then_inc(s.wca_loaded, 16)
            sp.dma_start(m.wout[:, :, :], wout).then_inc(s.wout_loaded, 16)
            sp.wait_ge(s.v2_zeroed, 1)
            sp.wait_ge(s.setup_copied, 2)
            for h in range(HEADS):
                for t in range(T):
                    sp.dma_start(m.v2blk[h * T + t:h * T + t + 1, :, h * D:(h + 1) * D],
                                 m.v2[t:128:T, h * D:(h + 1) * D]).then_inc(s.v2_placed, 16)

            def step(i, u, ahead, attend, ending):
                b = 2 * i + u
                if attend and ahead and not (isinstance(i, int) and b + 2 >= B):
                    sp.wait_ge(s.xT_made, b + 1)
                    sp.wait_ge(s.xb_made, b + 1)
                    sp.wait_ge(s.cT_made, b + 1)
                    load(i, u + 2)
                if ending:
                    sp.wait_ge(s.y_added, b)
                    sp.dma_start(out[bass.ds(b - 1, 1)].rearrange("b s h -> (b s) h"),
                                 m.y[:, (u - 1) % 2, :]).then_inc(stored[(u - 1) % 2], 16)

            run_batches(sp, step)
            sp.wait_ge(s.stored0, 16 * (B // 2))
            sp.wait_ge(s.stored1, 16 * (B // 2))

        @block.gpsimd
        def _(pool):
            g = nc.gpsimd
            g.memset(m.ident[:, :], 0.0).then_inc(s.ident_zeroed, 1)
            pool.wait_ge(s.ident_zeroed, 1)
            g.affine_select(out=m.ident[:, :], in_=m.ident[:, :], compare_op=ALU.not_equal, fill=1.0,
                            base=0, pattern=[[-1, 128]], channel_multiplier=1).then_inc(s.ident_made, 1)
            g.memset(m.zero[:, :], 0.0).then_inc(s.zero_made, 1)
            g.memset(m.v[:, :, :, D:D + 1], 1.0).then_inc(s.ones_v, 1)
            g.memset(m.xe[:, :, :, D:D + 1], 1.0).then_inc(s.ones_x, 1)
            g.memset(m.v2blk[:, :, :], 0.0).then_inc(s.v2_zeroed, 1)
            pool.wait_ge(s.ca_loaded, 2 * NM * 16)
            g.tensor_copy(m.ca_raw[:, :, CAD - 2:CAD - 1], m.ca_raw[:, :, CAD - 1:CAD]).then_inc(s.ca_fixed, 1)
            pool.wait_ge(s.ca_fixed, 1)
            pool.wait_ge(s.small_loaded, 32)
            pool.wait_ge(s.zero_made, 1)

            def pairs(t):
                return t.rearrange("p (n r) -> p n r", r=2)

            def column(t, n):
                return t.to_broadcast([128, n])

            def step(i, u, ahead, attend, ending):
                b = 2 * i + u
                if not ahead:
                    return
                nxt = (u + 1) % 2
                rows = m.ca_raw[:, bass.ds(b + 1, 1), :].rearrange("p b (n r) -> p (b n) r", r=3)[:, :, 0:2]
                g.tensor_copy(pairs(m.c_gath[:, :]), rows).then_inc(s.c_step, 1)
                pool.wait_ge(s.c_step, 6 * (b + 1) + 1)
                g.tensor_tensor(m.c_hi[:, :], m.c_gath[:, :], column(m.zero[:, :], S), ALU.add
                                ).then_inc(s.c_step, 1)
                pool.wait_ge(s.c_step, 6 * (b + 1) + 2)
                g.tensor_tensor(m.c_tmp[:, :], m.c_hi[:, :], column(m.signs[:, 2:3], S), ALU.mult
                                ).then_inc(s.c_step, 1)
                pool.wait_ge(s.c_step, 6 * (b + 1) + 3)
                g.tensor_tensor(m.c_res[:, :], m.c_gath[:, :], m.c_tmp[:, :], ALU.add).then_inc(s.c_step, 1)
                pool.wait_ge(s.c_step, 6 * (b + 1) + 4)
                g.tensor_tensor(m.c_mid[:, :], m.c_res[:, :], column(m.zero[:, :], S), ALU.add
                                ).then_inc(s.c_step, 1)
                pool.wait_ge(s.c_step, 6 * (b + 1) + 5)
                g.tensor_tensor(m.c_tmp2[:, :], m.c_mid[:, :], column(m.signs[:, 3:4], S), ALU.mult
                                ).then_inc(s.c_step, 1)
                pool.wait_ge(s.c_step, 6 * (b + 1) + 6)
                wait(pool, s.s_made, UNITS * b)
                g.tensor_tensor(m.c_st[:, nxt, :], m.c_res[:, :], m.c_tmp2[:, :], ALU.add
                                ).then_inc(s.c_stacked, 1)
                xn = m.x[:, nxt, :]
                pool.wait_ge(x_loaded[nxt], 16 * (i + (u + 1) // 2 + 1))
                wait(pool, s.pv_made, UNITS * b)
                g.tensor_tensor(m.xe[:, nxt, :, 0:D], xn.rearrange("p (h d) -> p h d", h=HEADS),
                                m.zero[:, :].unsqueeze(2).to_broadcast([128, HEADS, D]), ALU.add
                                ).then_inc(s.xe_copied, 1)
                wait(pool, s.y_added, b)
                g.tensor_tensor(m.xb[:, nxt, :], xn, m.bias[:, :], ALU.add).then_inc(s.xb_made, 1)

            run_batches(pool, step)

        @block.tensor
        def _(pe):
            mm = nc.tensor.matmul

            def three_transposes(dst, src):
                for k in range(NX):
                    last = nc.tensor.transpose(dst[0:XR, k * 128:(k + 1) * 128],
                                               src[:, X_AT[k]:X_AT[k] + XR], m.ident[:, :])
                return last

            def project_padded(dst, w, act, n_rows, n, chunks):
                for ch in chunks:
                    for k in range(n_rows):
                        last = mm(dst[:, ch * 128:ch * 128 + n], w[:, k, ch, :], act[:, k, 0:n],
                                  start=(k == 0), stop=(k == n_rows - 1))
                return last

            def scores(i, u, unit):
                b, slot = 2 * i + u, unit % 2
                at = slice(SLOT * slot, SLOT * slot + (D if unit < 2 else SLOT))
                if unit == 0:
                    pe.wait_ge(s.kT_copied, b + 1)
                    pe.wait_ge(s.qT_copied, b + 1)
                if unit == 2:
                    pe.wait_ge(s.m_stacked, b + 1)
                    pe.wait_ge(s.c_stacked, b + 1)
                wait(pe, s.shifted, UNITS * b + unit - 1)
                n = SE if unit < 2 else S
                for ch in range(NC):
                    dst = m.s_bank[unit % 2][:, ch * n:(ch + 1) * n]
                    if unit < 2:
                        last = mm(dst, m.qT[at, ch, :], m.kT[at, ch, :], start=True, stop=True)
                    else:
                        last = mm(dst, m.c_st[at, u % 2, :], m.m_st[at, ch, :], start=True, stop=True)
                last.then_inc(s.s_made, 1)

            def transpose_scores(i, u, unit):
                b = 2 * i + u
                n = SE if unit < 2 else S
                pe.wait_ge(s.shifted, UNITS * b + unit + 1)
                wait(pe, s.exped, UNITS * b + unit)
                for ch in range(NC):
                    last = nc.tensor.transpose(m.st_bank[0:n, ch * 128:(ch + 1) * 128],
                                               m.shift[:, unit % 2, ch, 0:n], m.ident[:, :])
                last.then_inc(s.st_made, 1)

            def apply_probs(i, u, unit):
                b, slot = 2 * i + u, unit % 2
                if unit == 0:
                    pe.wait_ge(s.v_copied, b + 1)
                if unit == 2:
                    pe.wait_ge(s.xe_copied, b + 1)
                pe.wait_ge(s.exped, UNITS * b + unit + 1)
                wait(pe, s.normed, UNITS * b + unit)
                for ch in range(NC):
                    dst = m.pv_bank[:, ch * (D + 1):(ch + 1) * (D + 1)]
                    if unit < 2:
                        last = mm(dst, m.p[0:SE, ch, :], m.v[:, u % 2, 2 * ch + slot, :], start=True, stop=True)
                    else:
                        last = mm(dst, m.p[:, ch, :], m.xe[:, u % 2, 2 * ch + slot, :], start=True, stop=True)
                last.then_inc(s.pv_made, 1)

            def setup():
                def item(n):
                    if n >= 4:
                        pe.wait_ge(s.setup_copied, n - 3)
                    return m.ring[n % 4]

                pe.wait_ge(s.v_copied, 2)
                pe.wait_ge(s.kT_copied, 2)
                pe.wait_ge(s.m_hi_made, 2)
                pe.wait_ge(s.m_res_made, 2)
                pe.wait_ge(s.ca_nat_loaded, 16)
                r = item(0)
                for k in range(NK):
                    last = nc.tensor.transpose(r[0:CR, k * 128:(k + 1) * 128],
                                               m.ca_nat[:, k * CR:(k + 1) * CR], m.ident[:, :])
                last.then_inc(s.setup_made, 1)
                r = item(1)
                pe.wait_ge(s.wca_loaded, 32)
                pe.wait_ge(s.setup_copied, 1)
                for k in range(NK):
                    last = mm(r[:, 0:H], m.caT[:, k, :], m.wvca[:, k, :], start=(k == 0), stop=(k == NK - 1))
                last.then_inc(s.setup_made, 1)
                r = item(2)
                project_padded(r, m.wkca, m.caT, NK, 128, range(NC)).then_inc(s.setup_made, 1)
                for k in range(NX):
                    r = item(3 + k)
                    for ch in range(NC):
                        last = nc.tensor.transpose(r[:, ch * XR:(ch + 1) * XR], m.wqs[:, k, ch, :],
                                                   m.ident[0:XR, 0:XR])
                    last.then_inc(s.setup_made, 1)
                pe.wait_ge(s.setup_copied, 6)
                for k in range(NX):
                    for slot in range(2):
                        r = item(6 + 2 * k + slot)
                        at = slice(SLOT * slot, SLOT * slot + D)
                        for ch in range(NC):
                            last = mm(r[0:XR, ch * 128:(ch + 1) * 128], m.wqT[at, k, ch, :], m.k2T[at, ch, :],
                                      start=True, stop=True)
                        last.then_inc(s.setup_made, 1)
                pe.wait_ge(s.setup_copied, 12)
                pe.wait_ge(s.v2_placed, 16 * HEADS * T)

            def step(i, u, ahead, attend, ending):
                b, nxt = 2 * i + u, (u + 1) % 2
                r = m.ring
                if attend:
                    scores(i, u, 1)
                if ahead:
                    pe.wait_ge(x_loaded[nxt], 16 * (i + (u + 1) // 2 + 1))
                    three_transposes(r[0], m.x[:, nxt, :]).then_inc(s.xT_made, 1)
                    pe.wait_ge(c_loaded[nxt], 16 * (i + (u + 1) // 2 + 1))
                    wait(pe, s.v_copied, b + 1)
                    for k in range(NK):
                        last = nc.tensor.transpose(r[1][0:CR, k * 128:(k + 1) * 128],
                                                   m.c[:, nxt, k * CR:(k + 1) * CR], m.ident[:, :])
                    last.then_inc(s.cT_made, 1)
                if attend:
                    transpose_scores(i, u, 0)
                if ending:
                    pe.wait_ge(s.normed, UNITS * b)
                    wait(pe, s.y_added, b - 1)
                    three_transposes(r[2], m.ca[:, :]).then_inc(s.aT_made, 1)
                if ahead:
                    pe.wait_ge(s.cT_copied, b + 2)
                    project_padded(r[3], m.wk, m.cT, NK, SE, range(0, 2))
                if attend:
                    apply_probs(i, u, 0)
                    scores(i, u, 2)
                if ahead:
                    project_padded(r[3], m.wk, m.cT, NK, SE, range(2, 4)).then_inc(s.kT_made, 1)
                if attend:
                    transpose_scores(i, u, 1)
                if ahead:
                    for k in range(NK):
                        last = mm(r[1][0:SE, 0:H], m.cT[:, k, 0:SE], m.wv[:, k, :], start=(k == 0), stop=(k == NK - 1))
                    last.then_inc(s.v_made, 1)
                if attend:
                    apply_probs(i, u, 1)
                    scores(i, u, 3)
                if ending:
                    pe.wait_ge(s.aT_copied, b)
                    if ahead:
                        pe.wait_ge(s.xT_copied, b + 2)
                    for k in range(NX):
                        last = mm(r[0][:, 0:HEADS * T], m.aT[:, k, :],
                                  m.g[:, k, bass.ds(b - 1, 1), :].rearrange("p b n -> p (b n)"),
                                  start=(k == 0), stop=(k == NX - 1))
                    last.then_inc(s.s3_made, 1)
                if ahead:
                    pe.wait_ge(s.xT_copied, b + 2)
                    project_padded(r[2], m.wqs, m.xT, NX, 128, range(0, 2))
                if attend:
                    transpose_scores(i, u, 2)
                if ahead:
                    project_padded(r[2], m.wqs, m.xT, NX, 128, range(2, 4)).then_inc(s.qT_made, 1)
                if ending:
                    pe.wait_ge(s.p3n_made, b)
                    if ahead:
                        pe.wait_ge(s.kT_copied, b + 2)
                    nc.tensor.transpose(r[3][0:HEADS * T, 0:128], m.p3n[:, :], m.ident[:, :]).then_inc(s.p3T_made, 1)
                if attend:
                    apply_probs(i, u, 2)
                if ending:
                    pe.wait_ge(s.p3T_copied, b)
                    mm(r[0][:, 0:H], m.p3T[:, :], m.v2blk[:, bass.ds(b - 1, 1), :].rearrange("p b n -> p (b n)"),
                       start=True, stop=True).then_inc(s.o3_made, 1)
                if ahead:
                    scores(i, u + 1, 0)
                if ending:
                    pe.wait_ge(s.o_summed, b)
                    if ahead:
                        pe.wait_ge(s.v_copied, b + 2)
                    three_transposes(r[1], m.osum[:, :]).then_inc(s.oT_made, 1)
                if attend:
                    transpose_scores(i, u, 3)
                if ending:
                    pe.wait_ge(s.oT_copied, b)
                    if ahead:
                        pe.wait_ge(s.m_res_made, b + 2)
                        pe.wait_ge(s.m_hi_made, b + 2)
                    for k in range(NX):
                        last = mm(r[2][:, 0:H], m.oT[:, k, :], m.wout[:, k, :], start=(k == 0), stop=(k == NX - 1))
                    last.then_inc(s.y_made, 1)
                if attend:
                    apply_probs(i, u, 3)
                if isinstance(i, int) and b == 0:
                    setup()

            pe.wait_ge(s.ident_made, 1)
            pe.wait_ge(s.wk_loaded, 16)
            pe.wait_ge(s.wq_scaled, 1)
            pe.wait_ge(s.wv_loaded, 16)
            pe.wait_ge(s.wout_loaded, 16)
            pe.wait_ge(s.ones_v, 1)
            pe.wait_ge(s.ones_x, 1)
            run_batches(pe, step)

        @block.scalar
        def _(act):
            act.dma_start(m.wq[:, :, :, :], wq_pad).then_inc(s.wq_loaded, 16)
            act.dma_start(m.signs[:, :], signs).then_inc(s.small_loaded, 16)
            act.wait_ge(s.ca_zeroed, 1)
            for slot in range(2):
                for pair in range(NM):
                    at = SLOT * slot + D + T * pair
                    act.dma_start(m.ca_raw[at:at + T, :, :], c[:, SE:S, :].rearrange("b t n -> t b n")
                                  ).then_inc(s.ca_loaded, 16)

            def copy(dst, src, sem):
                nc.scalar.activation(dst, src, ACT.Copy).then_inc(sem, 1)

            def by_blocks(bank, rows, n, width=128):
                return bank[0:rows, 0:n * width].rearrange("p (k q) -> p k q", k=n)

            def exps(i, u, unit):
                b = 2 * i + u
                n = SE if unit < 2 else S
                act.wait_ge(s.st_made, UNITS * b + unit + 1)
                wait(act, s.pv_made, UNITS * b + unit)
                nc.scalar.activation(m.p[0:n, :, :], by_blocks(m.st_bank, n, NC), ACT.Exp).then_inc(s.exped, 1)

            def setup():
                act.wait_ge(s.setup_made, 1)
                copy(m.caT[:, :, :], by_blocks(m.ring[0], CR, NK), s.setup_copied)
                act.wait_ge(s.setup_made, 2)
                copy(m.v2[:, :], m.ring[1][:, 0:H], s.setup_copied)
                act.wait_ge(s.setup_made, 3)
                copy(m.k2T[:, :, :], by_blocks(m.ring[2], 128, NC), s.setup_copied)
                for k in range(NX):
                    act.wait_ge(s.setup_made, 4 + k)
                    copy(m.wqT[:, k, :, :], by_blocks(m.ring[(3 + k) % 4], 128, NC, XR), s.setup_copied)
                for k in range(NX):
                    for slot in range(2):
                        n = 6 + 2 * k + slot
                        act.wait_ge(s.setup_made, n + 1)
                        dst = m.g[:, k, :, :].rearrange("p b (c j t) -> p c b j t", c=NC, j=2)[:, :, :, slot, :]
                        src = m.ring[n % 4][0:XR, :].rearrange("p (c b t) -> p c b t", c=NC, b=B)
                        copy(dst, src, s.setup_copied)

            def step(i, u, ahead, attend, ending):
                b, nxt, r = 2 * i + u, (u + 1) % 2, m.ring
                if ahead:
                    act.wait_ge(s.xT_made, b + 2)
                    copy(m.xT[:, :, :], by_blocks(r[0], XR, NX), s.xT_copied)
                    act.wait_ge(s.cT_made, b + 2)
                    copy(m.cT[:, :, :], by_blocks(r[1], CR, NK), s.cT_copied)
                if attend:
                    exps(i, u, 0)
                if ending:
                    act.wait_ge(s.aT_made, b)
                    copy(m.aT[:, :, :], by_blocks(r[2], XR, NX), s.aT_copied)
                if ahead:
                    act.wait_ge(s.kT_made, b + 2)
                    copy(m.kT[:, :, :], by_blocks(r[3], 128, NC)[:, :, 0:SE], s.kT_copied)
                if attend:
                    exps(i, u, 1)
                if ending:
                    act.wait_ge(s.sh3_made, b)
                    nc.scalar.activation(m.p3[:, :], m.sh3[:, :], ACT.Exp).then_inc(s.p3_made, 1)
                if attend:
                    exps(i, u, 2)
                if ahead:
                    act.wait_ge(s.qT_made, b + 2)
                    copy(m.qT[:, :, :], by_blocks(r[2], 128, NC), s.qT_copied)
                    copy(m.m_hi[:, :, :], by_blocks(r[2], 128, NC), s.m_hi_made)
                if ending:
                    act.wait_ge(s.oT_made, b)
                    copy(m.oT[:, :, :], by_blocks(r[1], XR, NX), s.oT_copied)
                if attend:
                    exps(i, u, 3)
                if ahead:
                    act.wait_ge(s.m_res_made, b + 2)
                    copy(m.m_mid[:, :, :], m.m_res[:, :, :], s.m_mid_made)
                if isinstance(i, int) and b == 0:
                    setup()

            run_batches(act, step)

        @block.vector
        def _(dve):
            v = nc.vector
            v.memset(m.ca_raw[:, :, :], 0.0).then_inc(s.ca_zeroed, 1)
            dve.wait_ge(s.wq_loaded, 16)
            v.tensor_scalar(m.wqs[:, :, :, :], m.wq[:, :, :, :], SCALE, None, ALU.mult).then_inc(s.wq_scaled, 1)
            dve.wait_ge(s.small_loaded, 32)

            def over(t, n):
                return t.unsqueeze(2).to_broadcast([t.shape[0], t.shape[1], n])

            def shift(i, u, unit):
                n, at = (SE if unit < 2 else S), UNITS * (2 * i + u) + unit
                src = m.s_bank[unit % 2][:, 0:NC * n].rearrange("p (c k) -> p c k", c=NC)
                dve.wait_ge(s.s_made, at + 1)
                v.tensor_reduce(m.smax[:, unit % 2, :], src, AX.X, ALU.max).then_inc(s.maxed, 1)
                dve.wait_ge(s.maxed, at + 1)
                wait(dve, s.st_made, at - 1)
                v.tensor_tensor(m.shift[:, unit % 2, :, 0:n], src, over(m.smax[:, unit % 2, :], n),
                                ALU.subtract).then_inc(s.shifted, 1)

            def normalise(i, u, unit):
                at = UNITS * (2 * i + u) + unit
                src = m.pv_bank[:, 0:NC * (D + 1)].rearrange("p (c d) -> p c d", c=NC)
                dve.wait_ge(s.pv_made, at + 1)
                v.reciprocal(m.rec[:, unit % 2, :], src[:, :, D]).then_inc(s.reced, 1)
                dve.wait_ge(s.reced, at + 1)
                dst = heads_of(m.hs[:, u % 2, :] if unit < 2 else m.ca[:, :], unit % 2)
                v.tensor_tensor(dst, src[:, :, 0:D], over(m.rec[:, unit % 2, :], D), ALU.mult
                                ).then_inc(s.normed, 1)

            def step(i, u, ahead, attend, ending):
                b, nxt, r = 2 * i + u, (u + 1) % 2, m.ring
                by_head = [m.sh3[:, :], m.p3[:, :], m.p3n[:, :], r[0][:, 0:HEADS * T]]
                sh3, p3, p3n, s3 = (t.rearrange("p (h t) -> p h t", h=HEADS) for t in by_head)
                if attend:
                    shift(i, u, 1)
                    normalise(i, u, 0)
                    shift(i, u, 2)
                if ahead:
                    dve.wait_ge(s.v_made, b + 2)
                    v.tensor_copy(m.v[:, nxt, :, 0:D], r[1][0:SE, 0:H].rearrange("p (h d) -> p h d", h=HEADS)
                                  ).then_inc(s.v_copied, 1)
                if attend:
                    normalise(i, u, 1)
                    shift(i, u, 3)
                if ending:
                    dve.wait_ge(s.s3_made, b)
                    v.tensor_reduce(m.max3[:, :], s3, AX.X, ALU.max).then_inc(s.max3_made, 1)
                    dve.wait_ge(s.max3_made, b)
                    v.tensor_tensor(sh3, s3, over(m.max3[:, :], T), ALU.subtract).then_inc(s.sh3_made, 1)
                    dve.wait_ge(s.p3_made, b)
                    v.tensor_reduce(m.sum3[:, :], p3, AX.X, ALU.add).then_inc(s.sum3_made, 1)
                    dve.wait_ge(s.sum3_made, b)
                    v.reciprocal(m.rec3[:, :], m.sum3[:, :]).then_inc(s.rec3_made, 1)
                    dve.wait_ge(s.rec3_made, b)
                    v.tensor_tensor(p3n, p3, over(m.rec3[:, :], T), ALU.mult).then_inc(s.p3n_made, 1)
                    dve.wait_ge(s.p3T_made, b)
                    v.tensor_copy(m.p3T[:, :], r[3][0:HEADS * T, 0:128]).then_inc(s.p3T_copied, 1)
                if attend:
                    normalise(i, u, 2)
                if ending:
                    dve.wait_ge(s.o3_made, b)
                    v.tensor_tensor(m.osum[:, :], r[0][:, 0:H], m.hs[:, (u - 1) % 2, :], ALU.add
                                    ).then_inc(s.o_summed, 1)
                if ahead:
                    dve.wait_ge(s.m_hi_made, b + 2)
                    v.scalar_tensor_tensor(m.m_res[:, :, :], m.m_hi[:, :, :], m.signs[:, 0:1],
                                           r[2][:, :].rearrange("p (c k) -> p c k", c=NC), ALU.mult, ALU.add
                                           ).then_inc(s.m_res_made, 1)
                    shift(i, u + 1, 0)
                if ending:
                    dve.wait_ge(s.y_made, b)
                    dve.wait_ge(s.xb_made, b)
                    wait(dve, stored[(u - 1) % 2], 16 * (i + (u - 1) // 2))
                    v.tensor_tensor(m.y[:, (u - 1) % 2, :], r[2][:, 0:H], m.xb[:, (u - 1) % 2, :], ALU.add
                                    ).then_inc(s.y_added, 1)
                if attend:
                    normalise(i, u, 3)
                if ahead:
                    dve.wait_ge(s.m_mid_made, b + 2)
                    v.scalar_tensor_tensor(m.m_st[:, :, :], m.m_mid[:, :, :], m.signs[:, 1:2], m.m_res[:, :, :],
                                           ALU.mult, ALU.add).then_inc(s.m_stacked, 1)

            run_batches(dve, step)


def kernel(x, ctx_768, L0_xattn_Wq, L0_xattn_Wk, L0_xattn_Wv, L0_xattn_Wq_ca, L0_xattn_Wk_ca, L0_xattn_Wv_ca,
           L0_xattn_Wout, L0_xattn_b_out):
    import numpy as np
    import concourse.bacc as bacc
    from concourse.bass_utils import run_bass_kernel_spmd

    f = np.float32
    wq, wk, wv, wq_ca, wk_ca, wv_ca, wout, bias = (np.asarray(a) for a in (
        L0_xattn_Wq, L0_xattn_Wk, L0_xattn_Wv, L0_xattn_Wq_ca, L0_xattn_Wk_ca, L0_xattn_Wv_ca, L0_xattn_Wout,
        L0_xattn_b_out))

    def padded(w, rows, n):
        out = np.zeros((rows, n, NC, 2, SLOT), f)
        out[..., 0:D] = w.reshape(n, rows, NC, 2, D).transpose(1, 0, 2, 3, 4)
        return out

    def by_threes(w):
        out = np.zeros((NX, XR) + w.shape[1:], f)
        out[0], out[1] = w[0:XR], w[XR:2 * XR]
        out[2, D:] = w[2 * XR:]
        return out

    wq_pad = padded(by_threes(wq).reshape(NX * XR, H), XR, NX)
    for h in range(HEADS):
        k, row = (h // 3, h % 3 * D) if h < 6 else (2, (h - 5) * D)
        for pair in range(NM):
            wq_pad[row:row + D, k, h // 2, h % 2, D + T * pair:D + T * (pair + 1)] = wq_ca[:, h * D:(h + 1) * D].T
    m_part, c_part = (0, 0, 1, 1, 0, 2), (0, 1, 0, 1, 2, 0)
    signs = np.zeros((2, SLOT, 4), f)
    for pair in range(NM):
        for col, part in ((0, m_part), (2, c_part)):
            signs[:, D + T * pair:D + T * (pair + 1), col] = -1.0 if part[pair] >= 1 else 0.0
            signs[:, D + T * pair:D + T * (pair + 1), col + 1] = -1.0 if part[pair] == 2 else 0.0

    def by_halves(w):
        return w.reshape(NK, CR, H).transpose(1, 0, 2)

    arrays = {
        "x": x, "c": ctx_768, "wq_pad": wq_pad.reshape(XR, NX, NC, 128),
        "wk_pad": padded(wk, CR, NK).reshape(CR, NK, NC, 128),
        "wkca_pad": padded(wk_ca, CR, NK).reshape(CR, NK, NC, 128),
        "wv": by_halves(wv), "wvca": by_halves(wv_ca), "wout": by_threes(wout).transpose(1, 0, 2),
        "bias": np.broadcast_to(bias, (128, H)), "signs": signs.reshape(128, 4),
    }
    arrays = {k: np.ascontiguousarray(a) for k, a in arrays.items()}
    nc = bacc.Bacc("TRN2", target_bir_lowering=False, num_devices=1)
    args = [nc.dram_tensor("in_" + k, a.shape, mybir.dt.float32, kind="ExternalInput").ap() for k, a in arrays.items()]
    out = nc.dram_tensor("out", (B, S, H), mybir.dt.float32, kind="ExternalOutput").ap()
    xattn_kernel(nc, *args, out)
    return run_bass_kernel_spmd(nc, [{"in_" + k: a for k, a in arrays.items()}], core_ids=[0]).results[0]["out"]
```

```python
import concourse.bass as bass
from concourse import mybir
from contextlib import ExitStack

B, S, H, CAD, T, HEADS = 32, 128, 320, 192, 4, 8
D = H // HEADS
SE = S - T
NC = 4
SLOT = 64
HT = HEADS * T
XR, NX = 120, 3
X_AT = (0, XR, H - XR)
CR, NK = 96, 2
SCALE = float(D) ** -0.5
UNITS = 4
KEY_PARTS = (0, 0, 0, 1, 1, 2)
QUERY_PARTS = (0, 1, 2, 0, 1, 0)
NM = len(KEY_PARTS)


class Memory:
    pass


def tensors(nc, ctx):
    f32, f16, bf16 = mybir.dt.float32, mybir.dt.float16, mybir.dt.bfloat16
    m = Memory()

    def sb(name, shape, dt=f32):
        return ctx.enter_context(nc.sbuf_tensor(name, shape, dt))

    m.wq = sb("wq", [XR, NX, H + HT])
    m.wqs = sb("wqs", [XR, NX, H + HT])
    m.wk = sb("wk", [CR, NK, H])
    m.wv = sb("wv", [CR, NK, H])
    m.wout = sb("wout", [XR, NX, H])
    m.bias = sb("bias", [128, H])
    m.signs = sb("signs", [128, 2])
    m.ident = sb("ident", [128, 128])
    m.zero = sb("zero", [128, 1])
    m.wkca = sb("wkca", [CR, NK, NC, 128])
    m.wvca = sb("wvca", [CR, NK, H])
    m.wqT = sb("wqT", [128, NX, NC, XR])
    m.caT = sb("caT", [CR, NK, B * T])
    m.k2T = sb("k2T", [128, NC, B * T])
    m.g = sb("g", [XR, NX, B, HT])
    m.v2 = sb("v2", [B * T, H])
    m.v2blk = sb("v2blk", [HT, B, H])
    m.x = sb("x", [128, 2, H])
    m.xT = sb("xT", [XR, 2, NX, 128])
    m.cT = sb("cT", [CR, 2, NK, 128])
    m.x_hi = sb("x_hi", [128, 2, HEADS, D + 1], bf16)
    m.x_mid = sb("x_mid", [128, 2, HEADS, D + 1], bf16)
    m.x_lo = sb("x_lo", [128, 2, HEADS, D + 1], bf16)
    m.x_res = sb("x_res", [128, H])
    m.xb = sb("xb", [128, 2, H])
    m.v_hi = sb("v_hi", [SE, 2, HEADS, D + 1], bf16)
    m.v_mid = sb("v_mid", [SE, 2, HEADS, D + 1], bf16)
    m.v_lo = sb("v_lo", [SE, 2, HEADS, D + 1], bf16)
    m.v_res = sb("v_res", [SE, H])
    m.k_nat = sb("k_nat", [SE, HEADS, SLOT])
    m.kT = sb("kT", [128, NC, SE])
    m.q_nat = sb("q_nat", [128, HEADS, SLOT])
    m.m_parts = sb("m_parts", [128, HEADS, NM, T], bf16)
    m.m_res = sb("m_res", [128, HT])
    m.qT = sb("qT", [128, NC, 128])
    m.m_st = sb("m_st", [128, NC, 128], bf16)
    m.c_raw = sb("c_raw", [128, 2, S])
    m.c_hi = sb("c_hi", [128, S], bf16)
    m.c_tmp = sb("c_tmp", [128, S])
    m.c_res = sb("c_res", [128, S])
    m.c_mid = sb("c_mid", [128, S], bf16)
    m.c_tmp2 = sb("c_tmp2", [128, S])
    m.c_st = sb("c_st", [128, 2, S], bf16)
    m.smax = sb("smax", [128, 2, NC])
    m.shift = sb("shift", [128, 2, NC, 128])
    m.p = sb("p", [128, NC, 128])
    m.p_hi = sb("p_hi", [128, 2, NC, 128], f16)
    m.p_lo = sb("p_lo", [128, 2, NC, 128], f16)
    m.rec = sb("rec", [128, 2, NC])
    m.hs = sb("hs", [128, 2, H])
    m.ca = sb("ca", [128, H])
    m.aT = sb("aT", [XR, NX, 128])
    m.max3 = sb("max3", [128, HEADS])
    m.sh3 = sb("sh3", [128, HT])
    m.p3 = sb("p3", [128, HT])
    m.sum3 = sb("sum3", [128, HEADS])
    m.rec3 = sb("rec3", [128, HEADS])
    m.p3n = sb("p3n", [128, HT])
    m.p3T = sb("p3T", [HT, 128])
    m.osum = sb("osum", [128, H])
    m.oT = sb("oT", [XR, NX, 128])
    m.y = sb("y", [128, 2, H])

    def bank(name):
        return ctx.enter_context(nc.psum_tensor(name, [128, 512], f32))

    m.s_bank = [bank("s_bank0"), bank("s_bank1")]
    m.st_bank = bank("st_bank")
    m.pv_bank = bank("pv_bank")
    m.ring = [bank(f"ring{r}") for r in range(4)]
    return m


class Semaphores:
    pass


def semaphores(nc, ctx):
    def sem(name):
        return ctx.enter_context(nc.semaphore(name))

    s = Semaphores()
    s.x_loaded0 = sem("x_loaded0")
    s.x_loaded1 = sem("x_loaded1")
    s.xT_loaded0 = sem("xT_loaded0")
    s.xT_loaded1 = sem("xT_loaded1")
    s.cT_loaded0 = sem("cT_loaded0")
    s.cT_loaded1 = sem("cT_loaded1")
    s.c_loaded0 = sem("c_loaded0")
    s.c_loaded1 = sem("c_loaded1")
    s.wk_loaded = sem("wk_loaded")
    s.wv_loaded = sem("wv_loaded")
    s.wq_loaded = sem("wq_loaded")
    s.wout_loaded = sem("wout_loaded")
    s.small_loaded = sem("small_loaded")
    s.setup_loaded = sem("setup_loaded")
    s.ident_zeroed = sem("ident_zeroed")
    s.ident_made = sem("ident_made")
    s.zero_made = sem("zero_made")
    s.c_zeroed = sem("c_zeroed")
    s.k_zeroed = sem("k_zeroed")
    s.parts_ones = sem("parts_ones")
    s.v2_zeroed = sem("v2_zeroed")
    s.v2_placed = sem("v2_placed")
    s.wq_scaled = sem("wq_scaled")
    s.setup_made = sem("setup_made")
    s.setup_copied = sem("setup_copied")
    s.k_made = sem("k_made")
    s.v_made = sem("v_made")
    s.qm_made = sem("qm_made")
    s.kT_made = sem("kT_made")
    s.qT_made = sem("qT_made")
    s.s_made = sem("s_made")
    s.st_made = sem("st_made")
    s.pv_made = sem("pv_made")
    s.aT_made = sem("aT_made")
    s.s3_made = sem("s3_made")
    s.p3T_made = sem("p3T_made")
    s.o3_made = sem("o3_made")
    s.oT_made = sem("oT_made")
    s.y_made = sem("y_made")
    s.k_copied = sem("k_copied")
    s.kT_copied = sem("kT_copied")
    s.v_hi_made = sem("v_hi_made")
    s.v_res_made = sem("v_res_made")
    s.v_mid_made = sem("v_mid_made")
    s.v_split = sem("v_split")
    s.q_copied = sem("q_copied")
    s.m_hi_made = sem("m_hi_made")
    s.m_res_made = sem("m_res_made")
    s.m_mid_made = sem("m_mid_made")
    s.m_split = sem("m_split")
    s.m_placed = sem("m_placed")
    s.qT_copied = sem("qT_copied")
    s.m_stacked = sem("m_stacked")
    s.c_step = sem("c_step")
    s.c_stacked = sem("c_stacked")
    s.x_step = sem("x_step")
    s.x_split = sem("x_split")
    s.xb_made = sem("xb_made")
    s.maxed = sem("maxed")
    s.shifted = sem("shifted")
    s.exped = sem("exped")
    s.p_hi_made = sem("p_hi_made")
    s.p_split = sem("p_split")
    s.reced = sem("reced")
    s.normed = sem("normed")
    s.aT_copied = sem("aT_copied")
    s.max3_made = sem("max3_made")
    s.sh3_made = sem("sh3_made")
    s.p3_made = sem("p3_made")
    s.sum3_made = sem("sum3_made")
    s.rec3_made = sem("rec3_made")
    s.p3n_made = sem("p3n_made")
    s.p3T_copied = sem("p3T_copied")
    s.o_summed = sem("o_summed")
    s.oT_copied = sem("oT_copied")
    s.y_added = sem("y_added")
    s.stored0 = sem("stored0")
    s.stored1 = sem("stored1")
    return s


def wait(eng, sem, count):
    if not isinstance(count, int) or count > 0:
        eng.wait_ge(sem, count)


def live(i, u):
    return not isinstance(i, int) or 0 <= 2 * i + u < B


def run_batches(eng, step):
    first, last = 4, B - 3
    for b in range(-1, first):
        step(0, b)
    with eng.Fori(first // 2, (last + 1) // 2) as i:
        step(i, 0)
        step(i, 1)
    for b in range(last + 1, B + 2):
        step(0, b)


def xattn_kernel(nc, x, xT, cT, c_rows, caT, wq, wk, wv, wkca, wvca, wqT, wout, bias, signs, out):
    ACT, ALU, AX = mybir.ActivationFunctionType, mybir.AluOpType, mybir.AxisListType
    ctx = ExitStack()
    with ctx:
        m = tensors(nc, ctx)
        s = semaphores(nc, ctx)
        x_loaded, xT_loaded = (s.x_loaded0, s.x_loaded1), (s.xT_loaded0, s.xT_loaded1)
        cT_loaded, c_loaded = (s.cT_loaded0, s.cT_loaded1), (s.c_loaded0, s.c_loaded1)
        stored = (s.stored0, s.stored1)
        block = ctx.enter_context(nc.Block())

        def nth(i, u):
            return i + u // 2 + 1

        def by_head(t, n=HEADS):
            return t.rearrange("p (h d) -> p h d", h=n)

        @block.sync
        def _(sp):
            def one(t, i, u):
                return t[bass.ds(2 * i + u, 1)]

            def load_projected(i, u):
                k = u % 2
                sp.dma_start(m.cT[:, k, :, :], one(cT, i, u).rearrange("b p k s -> (b p) k s")
                             ).then_inc(cT_loaded[k], 16)
                sp.dma_start(m.xT[:, k, :, :], one(xT, i, u).rearrange("b p k s -> (b p) k s")
                             ).then_inc(xT_loaded[k], 16)

            def load_rows(i, u):
                k = u % 2
                for slot in range(2):
                    at = SLOT * slot + D
                    sp.dma_start(m.c_raw[at:at + NM * T, k, :], one(c_rows, i, u).rearrange("b p s -> (b p) s")
                                 ).then_inc(c_loaded[k], 16)

            def load_x(i, u):
                sp.dma_start(m.x[:, u % 2, :], one(x, i, u).rearrange("b s h -> (b s) h")
                             ).then_inc(x_loaded[u % 2], 16)

            sp.dma_start(m.wk[:, :, :], wk).then_inc(s.wk_loaded, 16)
            load_projected(0, 0)
            sp.dma_start(m.wv[:, :, :], wv).then_inc(s.wv_loaded, 16)
            load_x(0, 0)
            sp.wait_ge(s.c_zeroed, 1)
            load_rows(0, 0)
            load_projected(0, 1)
            load_rows(0, 1)
            load_x(0, 1)
            sp.dma_start(m.wout[:, :, :], wout).then_inc(s.wout_loaded, 16)

            def place_v2():
                sp.wait_ge(s.v2_zeroed, 1)
                sp.wait_ge(s.setup_copied, 1)
                for h in range(HEADS):
                    for t in range(T):
                        sp.dma_start(m.v2blk[h * T + t:h * T + t + 1, :, h * D:(h + 1) * D],
                                     m.v2[t:B * T:T, h * D:(h + 1) * D]).then_inc(s.v2_placed, 16)

            def step(i, u):
                b = 2 * i + u
                if live(i, u) and live(i, u + 2):
                    sp.wait_ge(s.v_made, b + 1)
                    sp.wait_ge(s.qm_made, b + 1)
                    load_projected(i, u + 2)
                    sp.wait_ge(s.c_stacked, b + 1)
                    load_rows(i, u + 2)
                if live(i, u - 2):
                    sp.wait_ge(s.y_added, b - 1)
                    sp.dma_start(one(out, i, u - 2).rearrange("b s h -> (b s) h"), m.y[:, u % 2, :]
                                 ).then_inc(stored[u % 2], 16)
                if live(i, u) and live(i, u + 2):
                    sp.wait_ge(s.xb_made, b + 1)
                    load_x(i, u + 2)
                if isinstance(i, int) and b == 0:
                    place_v2()

            run_batches(sp, step)
            sp.wait_ge(s.stored0, 16 * (B // 2))
            sp.wait_ge(s.stored1, 16 * (B // 2))

        @block.gpsimd
        def _(pool):
            g = nc.gpsimd
            g.memset(m.c_raw[:, :, :], 0.0).then_inc(s.c_zeroed, 1)
            g.memset(m.ident[:, :], 0.0).then_inc(s.ident_zeroed, 1)
            pool.wait_ge(s.ident_zeroed, 1)
            g.affine_select(out=m.ident[:, :], in_=m.ident[:, :], compare_op=ALU.not_equal, fill=1.0,
                            base=0, pattern=[[-1, 128]], channel_multiplier=1).then_inc(s.ident_made, 1)
            g.memset(m.zero[:, :], 0.0).then_inc(s.zero_made, 1)
            g.memset(m.k_nat[:, :, D:SLOT], 0.0).then_inc(s.k_zeroed, 1)
            for t, value in ((m.v_hi, 1.0), (m.v_mid, 0.0), (m.v_lo, 0.0), (m.x_hi, 1.0), (m.x_mid, 0.0),
                             (m.x_lo, 0.0)):
                g.memset(t[:, :, :, D:D + 1], value).then_inc(s.parts_ones, 1)
            g.memset(m.v2blk[:, :, :], 0.0).then_inc(s.v2_zeroed, 1)
            pool.wait_ge(s.small_loaded, 32)
            pool.wait_ge(s.zero_made, 1)

            def column(t, n):
                return t.to_broadcast([128, n])

            def stack_queries(i, u):
                b, k, at = 2 * i + u, u % 2, 5 * (2 * i + u)
                raw = m.c_raw[:, k, :]
                pool.wait_ge(c_loaded[k], 32 * nth(i, u))
                g.tensor_tensor(m.c_hi[:, :], raw, column(m.zero[:, :], S), ALU.add).then_inc(s.c_step, 1)
                pool.wait_ge(s.c_step, at + 1)
                g.tensor_tensor(m.c_tmp[:, :], m.c_hi[:, :], column(m.signs[:, 0:1], S), ALU.mult
                                ).then_inc(s.c_step, 1)
                pool.wait_ge(s.c_step, at + 2)
                g.tensor_tensor(m.c_res[:, :], raw, m.c_tmp[:, :], ALU.add).then_inc(s.c_step, 1)
                pool.wait_ge(s.c_step, at + 3)
                g.tensor_tensor(m.c_mid[:, :], m.c_res[:, :], column(m.zero[:, :], S), ALU.add
                                ).then_inc(s.c_step, 1)
                pool.wait_ge(s.c_step, at + 4)
                g.tensor_tensor(m.c_tmp2[:, :], m.c_mid[:, :], column(m.signs[:, 1:2], S), ALU.mult
                                ).then_inc(s.c_step, 1)
                pool.wait_ge(s.c_step, at + 5)
                wait(pool, s.s_made, UNITS * (b - 1))
                g.tensor_tensor(m.c_st[:, k, :], m.c_res[:, :], m.c_tmp2[:, :], ALU.add
                                ).then_inc(s.c_stacked, 1)

            def split_x(i, u):
                b, k = 2 * i + u, u % 2
                xn, res = by_head(m.x[:, k, :]), by_head(m.x_res[:, :])
                zero = m.zero[:, :].unsqueeze(2).to_broadcast([128, HEADS, D])
                hi, mid, lo = (t[:, k, :, 0:D] for t in (m.x_hi, m.x_mid, m.x_lo))
                pool.wait_ge(x_loaded[k], 16 * nth(i, u))
                wait(pool, s.pv_made, UNITS * (b - 1))
                g.tensor_tensor(hi, xn, zero, ALU.add).then_inc(s.x_step, 1)
                pool.wait_ge(s.x_step, 3 * b + 1)
                g.tensor_tensor(res, xn, hi, ALU.subtract).then_inc(s.x_step, 1)
                pool.wait_ge(s.x_step, 3 * b + 2)
                g.tensor_tensor(mid, res, zero, ALU.add).then_inc(s.x_step, 1)
                pool.wait_ge(s.x_step, 3 * b + 3)
                g.tensor_tensor(lo, res, mid, ALU.subtract).then_inc(s.x_split, 1)

            def step(i, u):
                b = 2 * i + u
                if live(i, u + 1):
                    stack_queries(i, u + 1)
                    pool.wait_ge(s.v_mid_made, b + 2)
                    g.tensor_tensor(m.v_lo[:, (u + 1) % 2, :, 0:D], by_head(m.v_res[:, :]),
                                    m.v_mid[:, (u + 1) % 2, :, 0:D], ALU.subtract).then_inc(s.v_split, 1)
                    split_x(i, u + 1)
                if live(i, u):
                    wait(pool, s.y_added, b - 1)
                    pool.wait_ge(x_loaded[u % 2], 16 * nth(i, u))
                    g.tensor_tensor(m.xb[:, u % 2, :], m.x[:, u % 2, :], m.bias[:, :], ALU.add
                                    ).then_inc(s.xb_made, 1)

            run_batches(pool, step)

        @block.tensor
        def _(pe):
            mm = nc.tensor.matmul
            r = m.ring

            def three_transposes(dst, src):
                for k in range(NX):
                    last = nc.tensor.transpose(dst[0:XR, k * 128:(k + 1) * 128],
                                               src[:, X_AT[k]:X_AT[k] + XR], m.ident[:, :])
                return last

            def pair_transposes(dst, src, rows):
                for ch in range(NC):
                    last = nc.tensor.transpose(dst[:, ch * 128:ch * 128 + rows],
                                               src[:, 2 * ch:2 * ch + 2, :].rearrange("p j d -> p (j d)"),
                                               m.ident[0:rows, 0:rows])
                return last

            def chain(dst, act, w, n):
                for k in range(n):
                    last = mm(dst, act(k), w(k), start=(k == 0), stop=(k == n - 1))
                return last

            def scores(i, u, unit):
                b, slot = 2 * i + u, unit % 2
                at = slice(SLOT * slot, SLOT * slot + (D if unit < 2 else SLOT))
                if unit == 0:
                    pe.wait_ge(s.kT_copied, b + 1)
                    pe.wait_ge(s.qT_copied, b + 1)
                if unit == 2:
                    pe.wait_ge(s.m_stacked, b + 1)
                    pe.wait_ge(s.c_stacked, b + 1)
                wait(pe, s.shifted, UNITS * b + unit - 1)
                n = SE if unit < 2 else S
                for ch in range(NC):
                    dst = m.s_bank[unit % 2][:, ch * n:(ch + 1) * n]
                    if unit < 2:
                        last = mm(dst, m.qT[at, ch, :], m.kT[at, ch, :], start=True, stop=True)
                    else:
                        last = mm(dst, m.c_st[at, u % 2, :], m.m_st[at, ch, :], start=True, stop=True)
                last.then_inc(s.s_made, 1)

            def transpose_scores(i, u, unit):
                b = 2 * i + u
                n = SE if unit < 2 else S
                pe.wait_ge(s.shifted, UNITS * b + unit + 1)
                wait(pe, s.p_hi_made, UNITS * b + unit)
                for ch in range(NC):
                    last = nc.tensor.transpose(m.st_bank[0:n, ch * 128:(ch + 1) * 128],
                                               m.shift[:, unit % 2, ch, 0:n], m.ident[:, :])
                last.then_inc(s.st_made, 1)

            def apply_probs(i, u, unit):
                b, slot = 2 * i + u, unit % 2
                if unit == 0:
                    pe.wait_ge(s.v_split, b + 1)
                if unit == 2:
                    pe.wait_ge(s.x_split, b + 1)
                pe.wait_ge(s.p_split, UNITS * b + unit + 1)
                wait(pe, s.normed, UNITS * b + unit)
                n = SE if unit < 2 else S
                hi, mid, lo = (m.v_hi, m.v_mid, m.v_lo) if unit < 2 else (m.x_hi, m.x_mid, m.x_lo)
                pairs = ((m.p_hi, hi), (m.p_hi, mid), (m.p_hi, lo), (m.p_lo, hi), (m.p_lo, mid))
                for ch in range(NC):
                    dst = m.pv_bank[:, ch * (D + 1):(ch + 1) * (D + 1)]
                    for k, (p, val) in enumerate(pairs):
                        last = mm(dst, p[0:n, unit % 2, ch, :], val[0:n, u % 2, 2 * ch + slot, :],
                                  start=(k == 0), stop=(k == len(pairs) - 1))
                last.then_inc(s.pv_made, 1)

            def setup():
                def item(n):
                    if n >= 4:
                        pe.wait_ge(s.setup_copied, n - 3)
                    return r[n % 4]

                pe.wait_ge(s.m_stacked, 2)
                pe.wait_ge(s.v_hi_made, 2)
                pe.wait_ge(s.v_res_made, 2)
                pe.wait_ge(s.setup_loaded, 64)
                chain(item(0)[:, 0:H], lambda k: m.caT[:, k, :], lambda k: m.wvca[:, k, :], NK
                      ).then_inc(s.setup_made, 1)
                for ch in range(NC):
                    last = chain(item(1)[:, ch * 128:(ch + 1) * 128], lambda k: m.wkca[:, k, ch, :],
                                 lambda k: m.caT[:, k, :], NK)
                last.then_inc(s.setup_made, 1)
                pe.wait_ge(s.setup_copied, 2)
                for k in range(NX):
                    for slot in range(2):
                        dst = item(2 + 2 * k + slot)
                        at = slice(SLOT * slot, SLOT * slot + D)
                        for ch in range(NC):
                            last = mm(dst[0:XR, ch * 128:(ch + 1) * 128], m.wqT[at, k, ch, :], m.k2T[at, ch, :],
                                      start=True, stop=True)
                        last.then_inc(s.setup_made, 1)
                pe.wait_ge(s.setup_copied, 8)

            def step(i, u):
                b, nxt = 2 * i + u, (u + 1) % 2
                now, ahead = live(i, u), live(i, u + 1)
                before, finished = live(i, u - 1), live(i, u - 2)
                at_start = isinstance(i, int) and b == -1
                if now:
                    scores(i, u, 1)
                    pe.wait_ge(s.m_stacked, b + 1)
                if finished:
                    pe.wait_ge(s.o_summed, b - 1)
                    three_transposes(r[0], m.osum[:, :]).then_inc(s.oT_made, 1)
                if ahead:
                    if at_start:
                        pe.wait_ge(s.wk_loaded, 16)
                    pe.wait_ge(cT_loaded[nxt], 16 * nth(i, u + 1))
                    chain(r[1][0:SE, 0:H], lambda k: m.cT[:, nxt, k, 0:SE], lambda k: m.wk[:, k, :], NK
                          ).then_inc(s.k_made, 1)
                if now:
                    transpose_scores(i, u, 0)
                if before:
                    apply_probs(i, u - 1, 3)
                if now:
                    scores(i, u, 2)
                if ahead:
                    if at_start:
                        pe.wait_ge(s.wv_loaded, 16)
                    chain(r[3][0:SE, 0:H], lambda k: m.cT[:, nxt, k, 0:SE], lambda k: m.wv[:, k, :], NK
                          ).then_inc(s.v_made, 1)
                if now:
                    transpose_scores(i, u, 1)
                if ahead:
                    pe.wait_ge(s.k_copied, b + 2)
                    pair_transposes(r[0], m.k_nat, SE).then_inc(s.kT_made, 1)
                if now:
                    apply_probs(i, u, 0)
                if before:
                    pe.wait_ge(s.normed, UNITS * b)
                    three_transposes(r[1], m.ca[:, :]).then_inc(s.aT_made, 1)
                if now:
                    scores(i, u, 3)
                if ahead:
                    if at_start:
                        pe.wait_ge(s.wq_scaled, 1)
                    pe.wait_ge(xT_loaded[nxt], 16 * nth(i, u + 1))
                    chain(r[2][:, 0:H + HT], lambda k: m.xT[:, nxt, k, :], lambda k: m.wqs[:, k, :], NX
                          ).then_inc(s.qm_made, 1)
                if now:
                    transpose_scores(i, u, 2)
                if before:
                    pe.wait_ge(s.aT_copied, b)
                    if ahead:
                        pe.wait_ge(s.v_hi_made, b + 2)
                        pe.wait_ge(s.v_res_made, b + 2)
                    chain(r[3][:, 0:HT], lambda k: m.aT[:, k, :],
                          lambda k: m.g[:, k, bass.ds(b - 1, 1), :].rearrange("p b n -> p (b n)"), NX
                          ).then_inc(s.s3_made, 1)
                if now:
                    apply_probs(i, u, 1)
                if finished:
                    if isinstance(i, int) and b == 2:
                        pe.wait_ge(s.wout_loaded, 16)
                    pe.wait_ge(s.oT_copied, b - 1)
                    if ahead:
                        pe.wait_ge(s.q_copied, b + 2)
                        pe.wait_ge(s.m_res_made, b + 2)
                    chain(r[2][:, 0:H], lambda k: m.oT[:, k, :], lambda k: m.wout[:, k, :], NX
                          ).then_inc(s.y_made, 1)
                if ahead:
                    pe.wait_ge(s.q_copied, b + 2)
                    pe.wait_ge(s.m_placed, b + 2)
                    pe.wait_ge(s.kT_copied, b + 2)
                    pair_transposes(r[0], m.q_nat, 128).then_inc(s.qT_made, 1)
                if before:
                    pe.wait_ge(s.p3n_made, b)
                    nc.tensor.transpose(r[1][0:HT, 0:128], m.p3n[:, :], m.ident[:, :]).then_inc(s.p3T_made, 1)
                if now:
                    transpose_scores(i, u, 3)
                    apply_probs(i, u, 2)
                if before:
                    pe.wait_ge(s.p3T_copied, b)
                    if isinstance(i, int) and b == 1:
                        pe.wait_ge(s.v2_placed, 16 * HT)
                    wait(pe, s.y_added, b - 1)
                    mm(r[2][:, 0:H], m.p3T[:, :], m.v2blk[:, bass.ds(b - 1, 1), :].rearrange("p b n -> p (b n)"),
                       start=True, stop=True).then_inc(s.o3_made, 1)
                if ahead:
                    scores(i, u + 1, 0)
                if isinstance(i, int) and b == 0:
                    setup()

            pe.wait_ge(s.ident_made, 1)
            pe.wait_ge(s.k_zeroed, 1)
            pe.wait_ge(s.parts_ones, 6)
            run_batches(pe, step)

        @block.scalar
        def _(act):
            act.dma_start(m.wq[:, :, :], wq).then_inc(s.wq_loaded, 16)
            act.dma_start(m.signs[:, :], signs).then_inc(s.small_loaded, 16)
            act.dma_start(m.bias[:, :], bias).then_inc(s.small_loaded, 16)
            for t, src in ((m.caT, caT), (m.wvca, wvca), (m.wkca, wkca), (m.wqT, wqT)):
                act.dma_start(t[:], src).then_inc(s.setup_loaded, 16)

            def copy(dst, src, sem, scale=1.0):
                nc.scalar.activation(dst, src, ACT.Copy, scale=scale).then_inc(sem, 1)

            def by_blocks(bank, rows, n, width=128):
                return bank[0:rows, 0:n * width].rearrange("p (k q) -> p k q", k=n)

            def exps(i, u, unit):
                at = UNITS * (2 * i + u) + unit
                n = SE if unit < 2 else S
                act.wait_ge(s.st_made, at + 1)
                wait(act, s.p_split, at)
                nc.scalar.activation(m.p[0:n, :, :], by_blocks(m.st_bank, n, NC), ACT.Exp).then_inc(s.exped, 1)
                wait(act, s.pv_made, at - 1)
                nc.scalar.activation(m.p_hi[0:n, unit % 2, :, :], by_blocks(m.st_bank, n, NC), ACT.Exp
                                     ).then_inc(s.p_hi_made, 1)

            def setup():
                act.wait_ge(s.setup_made, 1)
                copy(m.v2[:, :], m.ring[0][:, 0:H], s.setup_copied)
                act.wait_ge(s.setup_made, 2)
                copy(m.k2T[:, :, :], by_blocks(m.ring[1], 128, NC), s.setup_copied)
                for k in range(NX):
                    for slot in range(2):
                        n = 2 + 2 * k + slot
                        act.wait_ge(s.setup_made, n + 1)
                        dst = m.g[:, k, :, :].rearrange("p b (c j t) -> p c b j t", c=NC, j=2)[:, :, :, slot, :]
                        src = m.ring[n % 4][0:XR, :].rearrange("p (c b t) -> p c b t", c=NC, b=B)
                        copy(dst, src, s.setup_copied, scale=SCALE)

            def step(i, u):
                b, nxt, r = 2 * i + u, (u + 1) % 2, m.ring
                now, ahead = live(i, u), live(i, u + 1)
                before, finished = live(i, u - 1), live(i, u - 2)
                if finished:
                    act.wait_ge(s.oT_made, b - 1)
                    copy(m.oT[:, :, :], by_blocks(r[0], XR, NX), s.oT_copied)
                if ahead:
                    act.wait_ge(s.k_made, b + 2)
                    copy(m.k_nat[:, :, 0:D], by_head(r[1][0:SE, 0:H]), s.k_copied)
                if now:
                    exps(i, u, 0)
                if ahead:
                    act.wait_ge(s.v_made, b + 2)
                    copy(m.v_hi[:, nxt, :, 0:D], by_head(r[3][0:SE, 0:H]), s.v_hi_made)
                if now:
                    exps(i, u, 1)
                if ahead:
                    act.wait_ge(s.kT_made, b + 2)
                    copy(m.kT[:, :, :], by_blocks(r[0], 128, NC)[:, :, 0:SE], s.kT_copied)
                    act.wait_ge(s.v_res_made, b + 2)
                    copy(m.v_mid[:, nxt, :, 0:D], by_head(m.v_res[:, :]), s.v_mid_made)
                if before:
                    act.wait_ge(s.aT_made, b)
                    copy(m.aT[:, :, :], by_blocks(r[1], XR, NX), s.aT_copied)
                if ahead:
                    act.wait_ge(s.qm_made, b + 2)
                    keys = by_head(r[2][:, H:H + HT]).unsqueeze(2)
                    copy(m.m_parts[:, :, 0:3, :], keys.to_broadcast([128, HEADS, 3, T]), s.m_hi_made)
                    copy(m.q_nat[:, :, 0:D], by_head(r[2][:, 0:H]), s.q_copied)
                if now:
                    exps(i, u, 2)
                if ahead:
                    act.wait_ge(s.m_res_made, b + 2)
                    copy(m.m_parts[:, :, 3:5, :], by_head(m.m_res[:, :]).unsqueeze(2).to_broadcast([128, HEADS, 2, T]),
                         s.m_mid_made)
                if before:
                    act.wait_ge(s.sh3_made, b)
                    nc.scalar.activation(m.p3[:, :], m.sh3[:, :], ACT.Exp).then_inc(s.p3_made, 1)
                if ahead:
                    act.wait_ge(s.m_split, b + 2)
                    copy(m.q_nat[:, :, D:SLOT].rearrange("p h (n t) -> p h n t", n=NM), m.m_parts[:, :, :, :],
                         s.m_placed)
                if ahead:
                    act.wait_ge(s.qT_made, b + 2)
                    copy(m.qT[:, :, :], by_blocks(r[0], 128, NC), s.qT_copied)
                if before:
                    act.wait_ge(s.p3T_made, b)
                    copy(m.p3T[:, :], r[1][0:HT, 0:128], s.p3T_copied)
                if now:
                    exps(i, u, 3)
                if ahead:
                    copy(m.m_st[:, :, :], by_blocks(r[0], 128, NC), s.m_stacked)
                if isinstance(i, int) and b == 0:
                    setup()

            run_batches(act, step)

        @block.vector
        def _(dve):
            v = nc.vector
            r = m.ring
            dve.wait_ge(s.wq_loaded, 16)
            v.tensor_scalar(m.wqs[:, :, :], m.wq[:, :, :], SCALE, None, ALU.mult).then_inc(s.wq_scaled, 1)

            def over(t, n):
                return t.unsqueeze(2).to_broadcast([t.shape[0], t.shape[1], n])

            def shift(i, u, unit):
                n, at = (SE if unit < 2 else S), UNITS * (2 * i + u) + unit
                src = m.s_bank[unit % 2][:, 0:NC * n].rearrange("p (c k) -> p c k", c=NC)
                dve.wait_ge(s.s_made, at + 1)
                v.tensor_reduce(m.smax[:, unit % 2, :], src, AX.X, ALU.max).then_inc(s.maxed, 1)
                dve.wait_ge(s.maxed, at + 1)
                wait(dve, s.st_made, at - 1)
                v.tensor_tensor(m.shift[:, unit % 2, :, 0:n], src, over(m.smax[:, unit % 2, :], n),
                                ALU.subtract).then_inc(s.shifted, 1)

            def split_probs(i, u, unit):
                n, at = (SE if unit < 2 else S), UNITS * (2 * i + u) + unit
                dve.wait_ge(s.p_hi_made, at + 1)
                v.tensor_tensor(m.p_lo[0:n, unit % 2, :, :], m.p[0:n, :, :], m.p_hi[0:n, unit % 2, :, :],
                                ALU.subtract).then_inc(s.p_split, 1)

            def normalise(i, u, unit):
                at = UNITS * (2 * i + u) + unit
                src = m.pv_bank[:, 0:NC * (D + 1)].rearrange("p (c d) -> p c d", c=NC)
                dve.wait_ge(s.pv_made, at + 1)
                v.reciprocal(m.rec[:, unit % 2, :], src[:, :, D]).then_inc(s.reced, 1)
                dve.wait_ge(s.reced, at + 1)
                dst = (m.hs[:, u % 2, :] if unit < 2 else m.ca[:, :]).rearrange("p (c j d) -> p c j d", c=NC, j=2)
                v.tensor_tensor(dst[:, :, unit % 2, :], src[:, :, 0:D], over(m.rec[:, unit % 2, :], D), ALU.mult
                                ).then_inc(s.normed, 1)

            def step(i, u):
                b, nxt = 2 * i + u, (u + 1) % 2
                now, ahead = live(i, u), live(i, u + 1)
                before, finished = live(i, u - 1), live(i, u - 2)
                sh3, p3, p3n, s3 = (by_head(t) for t in (m.sh3[:, :], m.p3[:, :], m.p3n[:, :], r[3][:, 0:HT]))
                if now:
                    shift(i, u, 1)
                    split_probs(i, u, 0)
                if before:
                    normalise(i, u - 1, 3)
                if now:
                    shift(i, u, 2)
                if ahead:
                    wait(dve, s.v_split, b + 1)
                    dve.wait_ge(s.v_hi_made, b + 2)
                    v.tensor_tensor(by_head(m.v_res[:, :]), by_head(r[3][0:SE, 0:H]), m.v_hi[:, nxt, :, 0:D],
                                    ALU.subtract).then_inc(s.v_res_made, 1)
                if now:
                    split_probs(i, u, 1)
                    normalise(i, u, 0)
                if now:
                    shift(i, u, 3)
                if ahead:
                    dve.wait_ge(s.m_hi_made, b + 2)
                    dve.wait_ge(s.q_copied, b + 2)
                    v.tensor_tensor(by_head(m.m_res[:, :]), by_head(r[2][:, H:H + HT]), m.m_parts[:, :, 0, :],
                                    ALU.subtract).then_inc(s.m_res_made, 1)
                if before:
                    dve.wait_ge(s.s3_made, b)
                    v.tensor_reduce(m.max3[:, :], s3, AX.X, ALU.max).then_inc(s.max3_made, 1)
                    dve.wait_ge(s.max3_made, b)
                    v.tensor_tensor(sh3, s3, over(m.max3[:, :], T), ALU.subtract).then_inc(s.sh3_made, 1)
                if now:
                    split_probs(i, u, 2)
                if ahead:
                    dve.wait_ge(s.m_mid_made, b + 2)
                    v.tensor_tensor(m.m_parts[:, :, 5, :], by_head(m.m_res[:, :]), m.m_parts[:, :, 3, :],
                                    ALU.subtract).then_inc(s.m_split, 1)
                if before:
                    dve.wait_ge(s.p3_made, b)
                    v.tensor_reduce(m.sum3[:, :], p3, AX.X, ALU.add).then_inc(s.sum3_made, 1)
                    dve.wait_ge(s.sum3_made, b)
                    v.reciprocal(m.rec3[:, :], m.sum3[:, :]).then_inc(s.rec3_made, 1)
                    dve.wait_ge(s.rec3_made, b)
                    v.tensor_tensor(p3n, p3, over(m.rec3[:, :], T), ALU.mult).then_inc(s.p3n_made, 1)
                if now:
                    normalise(i, u, 1)
                if finished:
                    dve.wait_ge(s.y_made, b - 1)
                    dve.wait_ge(s.xb_made, b - 1)
                    wait(dve, stored[u % 2], 16 * (nth(i, u - 2) - 1))
                    v.tensor_tensor(m.y[:, u % 2, :], r[2][:, 0:H], m.xb[:, u % 2, :], ALU.add
                                    ).then_inc(s.y_added, 1)
                if now:
                    split_probs(i, u, 3)
                    normalise(i, u, 2)
                if before:
                    dve.wait_ge(s.o3_made, b)
                    v.tensor_tensor(m.osum[:, :], r[2][:, 0:H], m.hs[:, (u - 1) % 2, :], ALU.add
                                    ).then_inc(s.o_summed, 1)
                if ahead:
                    shift(i, u + 1, 0)

            run_batches(dve, step)


def kernel(x, ctx_768, L0_xattn_Wq, L0_xattn_Wk, L0_xattn_Wv, L0_xattn_Wq_ca, L0_xattn_Wk_ca, L0_xattn_Wv_ca,
           L0_xattn_Wout, L0_xattn_b_out):
    import numpy as np
    import concourse.bacc as bacc
    from concourse.bass_utils import run_bass_kernel_spmd

    f = np.float32
    x, c, wq, wk, wv, wq_ca, wk_ca, wv_ca, wout, bias = (np.asarray(a) for a in (
        x, ctx_768, L0_xattn_Wq, L0_xattn_Wk, L0_xattn_Wv, L0_xattn_Wq_ca, L0_xattn_Wk_ca, L0_xattn_Wv_ca,
        L0_xattn_Wout, L0_xattn_b_out))

    def by_threes(w):
        out = np.zeros((XR, NX) + w.shape[1:], f)
        out[:, 0], out[:, 1], out[D:, 2] = w[0:XR], w[XR:2 * XR], w[2 * XR:]
        return out

    def by_halves(w):
        return w.reshape(NK, CR, -1).transpose(1, 0, 2)

    wq_and_ca = np.zeros((H, H + HT), f)
    wq_and_ca[:, 0:H] = wq
    wkca_pad = np.zeros((CR, NK, NC, 2, SLOT), f)
    wkca_pad[..., 0:D] = by_halves(wk_ca).reshape(CR, NK, NC, 2, D)
    wqT = np.zeros((2, SLOT, NX, NC, XR), f)
    wqT[:, 0:D] = by_threes(wq).reshape(XR, NX, NC, 2, D).transpose(3, 4, 1, 2, 0)
    signs = np.zeros((2, SLOT, 2), f)
    for h in range(HEADS):
        wq_and_ca[h * D:(h + 1) * D, H + h * T:H + (h + 1) * T] = wq_ca[:, h * D:(h + 1) * D].T
    for n, part in enumerate(QUERY_PARTS):
        signs[:, D + T * n:D + T * (n + 1), 0] = -1.0 if part >= 1 else 0.0
        signs[:, D + T * n:D + T * (n + 1), 1] = -1.0 if part == 2 else 0.0

    xt = x.transpose(0, 2, 1)
    xT = np.stack([xt[:, at:at + XR] for at in X_AT], axis=2)
    cT = c.transpose(0, 2, 1).reshape(B, NK, CR, S).transpose(0, 2, 1, 3)
    at = np.linspace(0, CAD - 1, S).astype(np.int64)
    c_rows = np.tile(c[:, SE:, at], (1, NM, 1))
    caT = by_halves(c[:, SE:, :].reshape(B * T, CAD).T)

    arrays = {
        "x": x, "xT": xT, "cT": cT, "c_rows": c_rows, "caT": caT, "wq": by_threes(wq_and_ca),
        "wk": by_halves(wk), "wv": by_halves(wv), "wkca": wkca_pad.reshape(CR, NK, NC, 128),
        "wvca": by_halves(wv_ca), "wqT": wqT.reshape(128, NX, NC, XR), "wout": by_threes(wout),
        "bias": np.broadcast_to(bias, (128, H)), "signs": signs.reshape(128, 2),
    }
    arrays = {f"in_{k}": np.ascontiguousarray(a) for k, a in arrays.items()}
    nc = bacc.Bacc("TRN2", target_bir_lowering=False, num_devices=1)
    args = [nc.dram_tensor(k, a.shape, mybir.dt.float32, kind="ExternalInput").ap() for k, a in arrays.items()]
    out = nc.dram_tensor("out", (B, S, H), mybir.dt.float32, kind="ExternalOutput").ap()
    xattn_kernel(nc, *args, out)
    return run_bass_kernel_spmd(nc, [arrays], core_ids=[0]).results[0]["out"]
```

```python
import concourse.bass as bass
from concourse import mybir
from contextlib import ExitStack

B, S, H, CAD, T, HEADS = 32, 128, 320, 192, 4, 8
D = H // HEADS
SE = S - T
NC = 4
SLOT = 64
HT = HEADS * T
NX, NK = 3, 2
XR = 120
X_AT = (0, XR, H - XR)
CR = 96
SCALE = float(D) ** -0.5
UNITS = 4
KEY_PARTS = (0, 0, 0, 1, 1, 2)
QUERY_PARTS = (0, 1, 2, 0, 1, 0)
NM = len(KEY_PARTS)
V2_PARTS = (0, 0, 1)
NP3 = len(V2_PARTS) * HT


class Memory:
    pass


def tensors(nc, ctx):
    f32, f16, bf16 = mybir.dt.float32, mybir.dt.float16, mybir.dt.bfloat16
    f32r = mybir.dt.float32r
    m = Memory()

    def sb(name, shape, dt=f32):
        return ctx.enter_context(nc.sbuf_tensor(name, shape, dt))

    m.wq = sb("wq", [128, NX, H + HT])
    m.wk = sb("wk", [128, NK, H])
    m.wv = sb("wv", [128, NK, H])
    m.wout = sb("wout", [128, NX, H])
    m.wq_h = sb("wq_h", [128, NX, H + HT], f32r)
    m.wq_l = sb("wq_l", [128, NX, H + HT], f32r)
    m.wk_h = sb("wk_h", [128, NK, H], f32r)
    m.wk_l = sb("wk_l", [128, NK, H], f32r)
    m.wv_h = sb("wv_h", [128, NK, H], f32r)
    m.wv_l = sb("wv_l", [128, NK, H], f32r)
    m.wout_h = sb("wout_h", [128, NX, H], f32r)
    m.wout_l = sb("wout_l", [128, NX, H], f32r)
    m.bias = sb("bias", [128, H])
    m.signs = sb("signs", [128, 2])
    m.ident = sb("ident", [128, 128])
    m.zero = sb("zero", [128, 1])
    m.wkca = sb("wkca", [CR, NK, NC, 128])
    m.wvca = sb("wvca", [CR, NK, H])
    m.wqT = sb("wqT", [128, NX, NC, XR])
    m.caT = sb("caT", [CR, NK, B * T])
    m.k2T = sb("k2T", [128, NC, B * T])
    m.g = sb("g", [XR, NX, B, HT])
    m.v2_h = sb("v2_h", [B * T, H], f32r)
    m.v2_l = sb("v2_l", [B * T, H], f32r)
    m.v2blk = sb("v2blk", [NP3, B, H], f32r)
    m.x = sb("x", [128, 2, H])
    m.xT = sb("xT", [128, 2, NX, 128])
    m.cT = sb("cT", [128, 2, NK, 128])
    m.x_h = sb("x_h", [128, 2, NX, 128], f32r)
    m.x_l = sb("x_l", [128, 2, NX, 128], f32r)
    m.c_h = sb("c_h", [128, 2, NK, 128], f32r)
    m.c_l = sb("c_l", [128, 2, NK, 128], f32r)
    m.x_hi = sb("x_hi", [128, 2, HEADS, D + 1], bf16)
    m.x_mid = sb("x_mid", [128, 2, HEADS, D + 1], bf16)
    m.x_lo = sb("x_lo", [128, 2, HEADS, D + 1], bf16)
    m.x_res = sb("x_res", [128, H])
    m.xb = sb("xb", [128, 2, H])
    m.v_hi = sb("v_hi", [SE, 2, HEADS, D + 1], bf16)
    m.v_mid = sb("v_mid", [SE, 2, HEADS, D + 1], bf16)
    m.v_lo = sb("v_lo", [SE, 2, HEADS, D + 1], bf16)
    m.v_nat = sb("v_nat", [SE, H])
    m.v_res = sb("v_res", [SE, H])
    m.k_nat = sb("k_nat", [SE, HEADS, SLOT])
    m.kT = sb("kT", [128, NC, SE])
    m.q_nat = sb("q_nat", [128, HEADS, SLOT])
    m.m_parts = sb("m_parts", [128, HEADS, NM, T], bf16)
    m.m_res = sb("m_res", [128, HT])
    m.qT = sb("qT", [128, NC, 128])
    m.m_st = sb("m_st", [128, NC, 128], bf16)
    m.c_raw = sb("c_raw", [128, 2, S])
    m.c_hi = sb("c_hi", [128, S], bf16)
    m.c_tmp = sb("c_tmp", [128, S])
    m.c_res = sb("c_res", [128, S])
    m.c_mid = sb("c_mid", [128, S], bf16)
    m.c_tmp2 = sb("c_tmp2", [128, S])
    m.c_st = sb("c_st", [128, 2, S], bf16)
    m.smax = sb("smax", [128, 2, NC])
    m.shift = sb("shift", [128, 2, NC, 128])
    m.p = sb("p", [128, 2, NC, 128])
    m.p_hi = sb("p_hi", [128, 2, NC, 128], f16)
    m.p_lo = sb("p_lo", [128, 2, NC, 128], f16)
    m.rec = sb("rec", [128, 2, NC])
    m.hs = sb("hs", [128, 2, H])
    m.ca = sb("ca", [128, H])
    m.aT = sb("aT", [XR, NX, 128])
    m.max3 = sb("max3", [128, HEADS])
    m.sh3 = sb("sh3", [128, HT])
    m.p3 = sb("p3", [128, HT])
    m.sum3 = sb("sum3", [128, HEADS])
    m.rec3 = sb("rec3", [128, HEADS])
    m.p3n = sb("p3n", [128, NP3])
    m.p3T = sb("p3T", [NP3, 128], f32r)
    m.osum = sb("osum", [128, NX * 128])
    m.o_h = sb("o_h", [128, NX, 128], f32r)
    m.o_l = sb("o_l", [128, NX - 1, 128], f32r)
    m.y = sb("y", [128, 2, H])

    def bank(name):
        return ctx.enter_context(nc.psum_tensor(name, [128, 512], f32))

    m.s_bank = [bank("s_bank0"), bank("s_bank1")]
    m.st_bank = bank("st_bank")
    m.pv_bank = bank("pv_bank")
    m.ring = [bank(f"ring{r}") for r in range(4)]
    return m


class Semaphores:
    pass


def semaphores(nc, ctx):
    def sem(name):
        return ctx.enter_context(nc.semaphore(name))

    s = Semaphores()
    s.x_loaded0 = sem("x_loaded0")
    s.x_loaded1 = sem("x_loaded1")
    s.xT_loaded0 = sem("xT_loaded0")
    s.xT_loaded1 = sem("xT_loaded1")
    s.cT_loaded0 = sem("cT_loaded0")
    s.cT_loaded1 = sem("cT_loaded1")
    s.c_loaded0 = sem("c_loaded0")
    s.c_loaded1 = sem("c_loaded1")
    s.wk_loaded = sem("wk_loaded")
    s.wv_loaded = sem("wv_loaded")
    s.wq_loaded = sem("wq_loaded")
    s.wout_loaded = sem("wout_loaded")
    s.signs_loaded = sem("signs_loaded")
    s.bias_loaded = sem("bias_loaded")
    s.setup_loaded = sem("setup_loaded")
    s.wqT_loaded = sem("wqT_loaded")
    s.ident_zeroed = sem("ident_zeroed")
    s.ident_made = sem("ident_made")
    s.zero_made = sem("zero_made")
    s.c_zeroed = sem("c_zeroed")
    s.k_zeroed = sem("k_zeroed")
    s.parts_ones = sem("parts_ones")
    s.v2_zeroed = sem("v2_zeroed")
    s.v2_split = sem("v2_split")
    s.v2_stored = sem("v2_stored")
    s.v2_placed = sem("v2_placed")
    s.w_zeroed = sem("w_zeroed")
    s.wk_rounded = sem("wk_rounded")
    s.wv_rounded = sem("wv_rounded")
    s.wq_rounded = sem("wq_rounded")
    s.wout_rounded = sem("wout_rounded")
    s.wk_split = sem("wk_split")
    s.wv_split = sem("wv_split")
    s.wq_split = sem("wq_split")
    s.wout_split = sem("wout_split")
    s.cT_hi_made = sem("cT_hi_made")
    s.cT_lo_made = sem("cT_lo_made")
    s.cT_split = sem("cT_split")
    s.xT_hi_made = sem("xT_hi_made")
    s.xT_lo_made = sem("xT_lo_made")
    s.xT_split = sem("xT_split")
    s.x_hi_made = sem("x_hi_made")
    s.o_hi_made = sem("o_hi_made")
    s.oT_split = sem("oT_split")
    s.setup_made = sem("setup_made")
    s.setup_copied = sem("setup_copied")
    s.k_made = sem("k_made")
    s.v_made = sem("v_made")
    s.qm_made = sem("qm_made")
    s.kT_made = sem("kT_made")
    s.qT_made = sem("qT_made")
    s.s_made = sem("s_made")
    s.st_made = sem("st_made")
    s.pv_made = sem("pv_made")
    s.aT_made = sem("aT_made")
    s.s3_made = sem("s3_made")
    s.p3T_made = sem("p3T_made")
    s.o3_made = sem("o3_made")
    s.oT_made = sem("oT_made")
    s.y_made = sem("y_made")
    s.k_copied = sem("k_copied")
    s.kT_copied = sem("kT_copied")
    s.v_hi_made = sem("v_hi_made")
    s.v_copied = sem("v_copied")
    s.v_res_made = sem("v_res_made")
    s.v_mid_made = sem("v_mid_made")
    s.v_split = sem("v_split")
    s.q_copied = sem("q_copied")
    s.m_hi_made = sem("m_hi_made")
    s.m_res_made = sem("m_res_made")
    s.m_mid_made = sem("m_mid_made")
    s.m_split = sem("m_split")
    s.m_placed = sem("m_placed")
    s.qT_copied = sem("qT_copied")
    s.m_stacked = sem("m_stacked")
    s.c_step = sem("c_step")
    s.c_stacked = sem("c_stacked")
    s.x_step = sem("x_step")
    s.x_split = sem("x_split")
    s.xb_made = sem("xb_made")
    s.maxed = sem("maxed")
    s.shifted = sem("shifted")
    s.exped = sem("exped")
    s.p_hi_made = sem("p_hi_made")
    s.p_split = sem("p_split")
    s.reced = sem("reced")
    s.normed = sem("normed")
    s.aT_copied = sem("aT_copied")
    s.max3_made = sem("max3_made")
    s.sh3_made = sem("sh3_made")
    s.p3_made = sem("p3_made")
    s.sum3_made = sem("sum3_made")
    s.rec3_made = sem("rec3_made")
    s.p3n_made = sem("p3n_made")
    s.p3T_copied = sem("p3T_copied")
    s.p3T_split = sem("p3T_split")
    s.o_summed = sem("o_summed")
    s.o_doubled = sem("o_doubled")
    s.y_added = sem("y_added")
    s.stored0 = sem("stored0")
    s.stored1 = sem("stored1")
    return s


def wait(eng, sem, count):
    if not isinstance(count, int) or count > 0:
        eng.wait_ge(sem, count)


def live(i, u):
    return not isinstance(i, int) or 0 <= 2 * i + u < B


def run_batches(eng, step):
    first, last = 4, B - 5
    for b in range(-1, first):
        step(0, b)
    with eng.Fori(first // 2, (last + 1) // 2) as i:
        step(i, 0)
        step(i, 1)
    for b in range(last + 1, B + 2):
        step(0, b)


def xattn_kernel(nc, x, xT, cT, c_rows, caT, wq, wk, wv, wkca, wvca, wqT, wout, bias, signs, out, v2_parts):
    ACT, ALU, AX = mybir.ActivationFunctionType, mybir.AluOpType, mybir.AxisListType
    ctx = ExitStack()
    with ctx:
        m = tensors(nc, ctx)
        s = semaphores(nc, ctx)
        x_loaded, xT_loaded = (s.x_loaded0, s.x_loaded1), (s.xT_loaded0, s.xT_loaded1)
        cT_loaded, c_loaded = (s.cT_loaded0, s.cT_loaded1), (s.c_loaded0, s.c_loaded1)
        stored = (s.stored0, s.stored1)
        block = ctx.enter_context(nc.Block())

        def nth(i, u):
            return i + u // 2 + 1

        def by_head(t, n=HEADS):
            return t.rearrange("p (h d) -> p h d", h=n)

        @block.sync
        def _(sp):
            def one(t, i, u):
                return t[bass.ds(2 * i + u, 1)]

            def load_projected(i, u):
                k = u % 2
                sp.dma_start(m.cT[:, k, :, :], one(cT, i, u).rearrange("b p k s -> (b p) k s")
                             ).then_inc(cT_loaded[k], 16)
                sp.dma_start(m.xT[:, k, :, :], one(xT, i, u).rearrange("b p k s -> (b p) k s")
                             ).then_inc(xT_loaded[k], 16)

            def load_rows(i, u):
                k = u % 2
                for slot in range(2):
                    at = SLOT * slot + D
                    sp.dma_start(m.c_raw[at:at + NM * T, k, :], one(c_rows, i, u).rearrange("b p s -> (b p) s")
                                 ).then_inc(c_loaded[k], 16)

            def load_x(i, u):
                sp.dma_start(m.x[:, u % 2, :], one(x, i, u).rearrange("b s h -> (b s) h")
                             ).then_inc(x_loaded[u % 2], 16)

            load_projected(0, 0)
            sp.dma_start(m.wv[:, :, :], wv).then_inc(s.wv_loaded, 16)
            load_projected(0, 1)
            load_x(0, 0)
            sp.dma_start(m.signs[:, :], signs).then_inc(s.signs_loaded, 16)
            sp.wait_ge(s.c_zeroed, 1)
            load_rows(0, 0)
            for t, src in ((m.caT, caT), (m.wvca, wvca), (m.wkca, wkca)):
                sp.dma_start(t[:], src).then_inc(s.setup_loaded, 16)
            load_x(0, 1)
            load_rows(0, 1)
            sp.dma_start(m.wqT[:], wqT).then_inc(s.wqT_loaded, 16)
            sp.dma_start(m.bias[:, :], bias).then_inc(s.bias_loaded, 16)
            sp.dma_start(m.wout[:, :, :], wout).then_inc(s.wout_loaded, 16)

            def place_v2():
                sp.wait_ge(s.setup_copied, 1)
                sp.dma_start(v2_parts[0], m.v2_h[:, :].bitcast(mybir.dt.float32)).then_inc(s.v2_stored, 16)
                sp.wait_ge(s.v2_split, 1)
                sp.dma_start(v2_parts[1], m.v2_l[:, :].bitcast(mybir.dt.float32)).then_inc(s.v2_stored, 16)
                sp.wait_ge(s.v2_zeroed, 4)
                sp.wait_ge(s.v2_stored, 32)
                for n, part in enumerate(V2_PARTS):
                    for h in range(HEADS):
                        at, cols = n * HT + h * T, slice(h * D, (h + 1) * D)
                        sp.dma_start(m.v2blk[at:at + T, :, cols].bitcast(mybir.dt.float32),
                                     v2_parts[part, :, cols].rearrange("(b t) d -> t b d", t=T)
                                     ).then_inc(s.v2_placed, 16)

            def step(i, u):
                b = 2 * i + u
                if live(i, u + 1) and live(i, u + 3):
                    sp.wait_ge(s.cT_split, b + 2)
                    sp.wait_ge(s.xT_split, b + 2)
                    load_projected(i, u + 3)
                if live(i, u) and live(i, u + 2):
                    sp.wait_ge(s.c_stacked, b + 1)
                    load_rows(i, u + 2)
                if isinstance(i, int) and b == 0:
                    place_v2()
                if live(i, u - 2):
                    sp.wait_ge(s.y_added, b - 1)
                    sp.dma_start(one(out, i, u - 2).rearrange("b s h -> (b s) h"), m.y[:, u % 2, :]
                                 ).then_inc(stored[u % 2], 16)
                if live(i, u) and live(i, u + 2):
                    sp.wait_ge(s.xb_made, b + 1)
                    load_x(i, u + 2)

            run_batches(sp, step)
            sp.wait_ge(s.stored0, 16 * (B // 2))
            sp.wait_ge(s.stored1, 16 * (B // 2))

        @block.gpsimd
        def _(pool):
            g = nc.gpsimd
            g.memset(m.c_raw[:, :, :], 0.0).then_inc(s.c_zeroed, 1)
            g.memset(m.ident[:, :], 0.0).then_inc(s.ident_zeroed, 1)
            pool.wait_ge(s.ident_zeroed, 1)
            g.affine_select(out=m.ident[:, :], in_=m.ident[:, :], compare_op=ALU.not_equal, fill=1.0,
                            base=0, pattern=[[-1, 128]], channel_multiplier=1).then_inc(s.ident_made, 1)
            g.memset(m.zero[:, :], 0.0).then_inc(s.zero_made, 1)
            g.memset(m.k_nat[:, :, D:SLOT], 0.0).then_inc(s.k_zeroed, 1)
            for t, value in ((m.v_hi, 1.0), (m.v_mid, 0.0), (m.v_lo, 0.0), (m.x_hi, 1.0), (m.x_mid, 0.0),
                             (m.x_lo, 0.0)):
                g.memset(t[:, :, :, D:D + 1], value).then_inc(s.parts_ones, 1)
            g.memset(m.v2blk[:, 0:B // 4, :].bitcast(mybir.dt.float32), 0.0).then_inc(s.v2_zeroed, 1)
            pool.wait_ge(s.zero_made, 1)

            def column(t, n):
                return t.to_broadcast([128, n])

            def stack_queries(i, u):
                b, k, at = 2 * i + u, u % 2, 5 * (2 * i + u)
                raw = m.c_raw[:, k, :]
                pool.wait_ge(c_loaded[k], 32 * nth(i, u))
                g.tensor_tensor(m.c_hi[:, :], raw, column(m.zero[:, :], S), ALU.add).then_inc(s.c_step, 1)
                pool.wait_ge(s.c_step, at + 1)
                g.tensor_tensor(m.c_tmp[:, :], m.c_hi[:, :], column(m.signs[:, 0:1], S), ALU.mult
                                ).then_inc(s.c_step, 1)
                pool.wait_ge(s.c_step, at + 2)
                g.tensor_tensor(m.c_res[:, :], raw, m.c_tmp[:, :], ALU.add).then_inc(s.c_step, 1)
                pool.wait_ge(s.c_step, at + 3)
                g.tensor_tensor(m.c_mid[:, :], m.c_res[:, :], column(m.zero[:, :], S), ALU.add
                                ).then_inc(s.c_step, 1)
                pool.wait_ge(s.c_step, at + 4)
                g.tensor_tensor(m.c_tmp2[:, :], m.c_mid[:, :], column(m.signs[:, 1:2], S), ALU.mult
                                ).then_inc(s.c_step, 1)
                pool.wait_ge(s.c_step, at + 5)
                wait(pool, s.s_made, UNITS * (b - 1))
                g.tensor_tensor(m.c_st[:, k, :], m.c_res[:, :], m.c_tmp2[:, :], ALU.add
                                ).then_inc(s.c_stacked, 1)

            def split_projected(i, u):
                b, k = 2 * i + u, u % 2
                wait(pool, s.v_made, b - 1)
                pool.wait_ge(s.cT_hi_made, b + 1)
                g.tensor_tensor(m.c_l[:, k, :, :], m.cT[:, k, :, :], m.c_h[:, k, :, :], ALU.subtract
                                ).then_inc(s.cT_lo_made, 1)
                pool.wait_ge(s.cT_lo_made, b + 1)
                g.tensor_tensor(m.c_h[SLOT:128, k, NK - 1, :], m.c_l[SLOT:128, k, NK - 1, :],
                                m.zero[SLOT:128, :].to_broadcast([128 - SLOT, S]), ALU.add).then_inc(s.cT_split, 1)
                pool.wait_ge(s.cT_split, b + 1)
                pool.wait_ge(s.xT_hi_made, b + 1)
                g.tensor_tensor(m.x_l[:, k, :, :], m.xT[:, k, :, :], m.x_h[:, k, :, :], ALU.subtract
                                ).then_inc(s.xT_lo_made, 1)
                pool.wait_ge(s.xT_lo_made, b + 1)
                g.tensor_tensor(m.x_h[SLOT:128, k, NX - 1, :], m.x_l[SLOT:128, k, NX - 1, :],
                                m.zero[SLOT:128, :].to_broadcast([128 - SLOT, S]), ALU.add).then_inc(s.xT_split, 1)
                pool.wait_ge(s.xT_split, b + 1)

            def split_x(i, u):
                b, k = 2 * i + u, u % 2
                xn, res = by_head(m.x[:, k, :]), by_head(m.x_res[:, :])
                zero = m.zero[:, :].unsqueeze(2).to_broadcast([128, HEADS, D])
                hi, mid, lo = (t[:, k, :, 0:D] for t in (m.x_hi, m.x_mid, m.x_lo))
                pool.wait_ge(s.x_hi_made, b + 1)
                g.tensor_tensor(res, xn, hi, ALU.subtract).then_inc(s.x_step, 1)
                pool.wait_ge(s.x_step, 2 * b + 1)
                g.tensor_tensor(mid, res, zero, ALU.add).then_inc(s.x_step, 1)
                pool.wait_ge(s.x_step, 2 * b + 2)
                g.tensor_tensor(lo, res, mid, ALU.subtract).then_inc(s.x_split, 1)

            split_projected(0, 0)
            g.memset(m.v2blk[:, B // 4:2 * B // 4, :].bitcast(mybir.dt.float32), 0.0).then_inc(s.v2_zeroed, 1)
            split_projected(0, 1)
            pool.wait_ge(s.signs_loaded, 16)

            def step(i, u):
                b = 2 * i + u
                if live(i, u + 1):
                    stack_queries(i, u + 1)
                if live(i, u + 2) and not (isinstance(i, int) and b == -1):
                    split_projected(i, u + 2)
                if live(i, u + 1):
                    split_x(i, u + 1)
                if live(i, u + 1):
                    pool.wait_ge(s.v_copied, b + 2)
                    g.tensor_tensor(by_head(m.v_res[:, :]), by_head(m.v_nat[:, :]),
                                    m.v_hi[:, (u + 1) % 2, :, 0:D], ALU.subtract).then_inc(s.v_res_made, 1)
                if live(i, u):
                    wait(pool, s.y_added, b - 1)
                    pool.wait_ge(x_loaded[u % 2], 16 * nth(i, u))
                    if isinstance(i, int) and b == 0:
                        pool.wait_ge(s.bias_loaded, 16)
                    g.tensor_tensor(m.xb[:, u % 2, :], m.x[:, u % 2, :], m.bias[:, :], ALU.add
                                    ).then_inc(s.xb_made, 1)
                if live(i, u + 1):
                    pool.wait_ge(s.v_mid_made, b + 2)
                    g.tensor_tensor(m.v_lo[:, (u + 1) % 2, :, 0:D], by_head(m.v_res[:, :]),
                                    m.v_mid[:, (u + 1) % 2, :, 0:D], ALU.subtract).then_inc(s.v_split, 1)

            run_batches(pool, step)

        @block.tensor
        def _(pe):
            mm = nc.tensor.matmul
            r = m.ring

            def three_transposes(dst, src):
                for k in range(NX):
                    last = nc.tensor.transpose(dst[0:XR, k * 128:(k + 1) * 128],
                                               src[:, X_AT[k]:X_AT[k] + XR], m.ident[:, :])
                return last

            def pair_transposes(dst, src, rows):
                for ch in range(NC):
                    last = nc.tensor.transpose(dst[:, ch * 128:ch * 128 + rows],
                                               src[:, 2 * ch:2 * ch + 2, :].rearrange("p j d -> p (j d)"),
                                               m.ident[0:rows, 0:rows])
                return last

            def chain(dst, act, w, n):
                for k in range(n):
                    last = mm(dst, act(k), w(k), start=(k == 0), stop=(k == n - 1))
                return last

            def split_chain(dst, act_h, act_l, w_h, w_l, n):
                for k in range(n):
                    mm(dst, act_h(k), w_h[:, k, :], start=(k == 0), stop=False)
                    last = mm(dst, act_h(k), w_l[:, k, :], start=False, stop=(k == n - 1))
                    if k < n - 1:
                        mm(dst, act_l(k), w_h[:, k, :], start=False, stop=False)
                return last

            def scores(i, u, unit):
                b, slot = 2 * i + u, unit % 2
                at = slice(SLOT * slot, SLOT * slot + (D if unit < 2 else SLOT))
                if unit == 0:
                    pe.wait_ge(s.kT_copied, b + 1)
                    pe.wait_ge(s.qT_copied, b + 1)
                if unit == 2:
                    pe.wait_ge(s.m_stacked, b + 1)
                    pe.wait_ge(s.c_stacked, b + 1)
                wait(pe, s.shifted, UNITS * b + unit - 1)
                bank = m.s_bank[unit % 2]
                if unit < 2:
                    for ch in range(NC):
                        last = mm(bank[:, ch * SE:(ch + 1) * SE], m.qT[at, ch, :], m.kT[at, ch, :],
                                  start=True, stop=True)
                else:
                    last = mm(bank[:, 0:NC * S], m.c_st[at, u % 2, :],
                              m.m_st[at, :, :].rearrange("p c k -> p (c k)"), start=True, stop=True)
                last.then_inc(s.s_made, 1)

            def transpose_scores(i, u, unit):
                b = 2 * i + u
                n = SE if unit < 2 else S
                pe.wait_ge(s.shifted, UNITS * b + unit + 1)
                wait(pe, s.p_hi_made, UNITS * b + unit)
                for ch in range(NC):
                    last = nc.tensor.transpose(m.st_bank[0:n, ch * 128:(ch + 1) * 128],
                                               m.shift[:, unit % 2, ch, 0:n], m.ident[:, :])
                last.then_inc(s.st_made, 1)

            def apply_probs(i, u, unit):
                b, slot = 2 * i + u, unit % 2
                if unit == 0:
                    pe.wait_ge(s.v_split, b + 1)
                if unit == 2:
                    pe.wait_ge(s.x_split, b + 1)
                pe.wait_ge(s.p_split, UNITS * b + unit + 1)
                wait(pe, s.normed, UNITS * b + unit)
                n = SE if unit < 2 else S
                hi, mid, lo = (m.v_hi, m.v_mid, m.v_lo) if unit < 2 else (m.x_hi, m.x_mid, m.x_lo)
                pairs = ((m.p_hi, hi), (m.p_hi, mid), (m.p_hi, lo), (m.p_lo, hi), (m.p_lo, mid))
                for ch in range(NC):
                    dst = m.pv_bank[:, ch * (D + 1):(ch + 1) * (D + 1)]
                    for k, (p, val) in enumerate(pairs):
                        last = mm(dst, p[0:n, unit % 2, ch, :], val[0:n, u % 2, 2 * ch + slot, :],
                                  start=(k == 0), stop=(k == len(pairs) - 1))
                last.then_inc(s.pv_made, 1)

            def last_rows_values():
                pe.wait_ge(s.setup_loaded, 48)
                pe.wait_ge(s.k_copied, 1)
                chain(r[1][:, 0:H], lambda k: m.caT[:, k, :], lambda k: m.wvca[:, k, :], NK
                      ).then_inc(s.setup_made, 1)

            def last_rows_keys():
                pe.wait_ge(s.q_copied, 1)
                pe.wait_ge(s.m_res_made, 1)
                for ch in range(NC):
                    last = chain(r[2][:, ch * 128:(ch + 1) * 128], lambda k: m.wkca[:, k, ch, :],
                                 lambda k: m.caT[:, k, :], NK)
                last.then_inc(s.setup_made, 1)

            def keys_behind_wq(n, ring):
                if n == 0:
                    pe.wait_ge(s.wqT_loaded, 16)
                    pe.wait_ge(s.setup_copied, 2)
                k, slot = n // 2, n % 2
                at = slice(SLOT * slot, SLOT * slot + D)
                for ch in range(NC):
                    last = mm(r[ring][0:XR, ch * 128:(ch + 1) * 128], m.wqT[at, k, ch, :], m.k2T[at, ch, :],
                              start=True, stop=True)
                last.then_inc(s.setup_made, 1)

            def step(i, u):
                b, nxt = 2 * i + u, (u + 1) % 2
                now, ahead = live(i, u), live(i, u + 1)
                before, finished = live(i, u - 1), live(i, u - 2)
                at_start = isinstance(i, int) and b == -1
                at_first = isinstance(i, int) and b == 0

                def put_out(bank):
                    if isinstance(i, int) and b == 2:
                        pe.wait_ge(s.wout_split, 2)
                    pe.wait_ge(s.oT_split, 2 * (b - 1))
                    if ahead:
                        pe.wait_ge(s.q_copied, b + 2)
                        pe.wait_ge(s.m_res_made, b + 2)
                    split_chain(bank[:, 0:H], lambda k: m.o_h[:, k, :], lambda k: m.o_l[:, k, :],
                                m.wout_h, m.wout_l, NX).then_inc(s.y_made, 1)

                alone = before and not now
                if alone:
                    apply_probs(i, u - 1, 3)
                if ahead:
                    if at_start:
                        pe.wait_ge(s.wk_split, 2)
                    pe.wait_ge(s.cT_split, b + 2)
                    if at_first:
                        pe.wait_ge(s.v2_split, 1)
                    if isinstance(i, int) and b == 1:
                        pe.wait_ge(s.setup_copied, 6)
                    split_chain(r[1][0:SE, 0:H], lambda k: m.c_h[:, nxt, k, 0:SE], lambda k: m.c_l[:, nxt, k, 0:SE],
                                m.wk_h, m.wk_l, NK).then_inc(s.k_made, 1)
                if before and now:
                    apply_probs(i, u - 1, 3)
                if now:
                    transpose_scores(i, u, 0)
                    scores(i, u, 2)
                if now:
                    pe.wait_ge(s.m_stacked, b + 1)
                if finished:
                    pe.wait_ge(s.o_summed, b - 1)
                    for k in range(NX):
                        if k == NX - 1:
                            pe.wait_ge(s.o_doubled, b - 1)
                        last = nc.tensor.transpose(r[0][:, k * 128:(k + 1) * 128],
                                                   m.osum[:, k * 128:(k + 1) * 128], m.ident[:, :])
                    last.then_inc(s.oT_made, 1)
                if at_first:
                    pe.wait_ge(s.v_copied, 1)
                    keys_behind_wq(0, 3)
                if isinstance(i, int) and b == 1:
                    pe.wait_ge(s.v_copied, 2)
                    keys_behind_wq(5, 3)
                    pe.wait_ge(s.setup_copied, 7)
                if ahead:
                    if at_start:
                        pe.wait_ge(s.wq_split, 2)
                    pe.wait_ge(s.xT_split, b + 2)
                    if finished:
                        pe.wait_ge(s.o_summed, b - 1)
                    split_chain(r[2][:, 0:H + HT], lambda k: m.x_h[:, nxt, k, :], lambda k: m.x_l[:, nxt, k, :],
                                m.wq_h, m.wq_l, NX).then_inc(s.qm_made, 1)
                if now:
                    transpose_scores(i, u, 1)
                    scores(i, u, 3)
                    apply_probs(i, u, 0)
                if before:
                    pe.wait_ge(s.normed, UNITS * b)
                    three_transposes(r[1], m.ca[:, :]).then_inc(s.aT_made, 1)
                if ahead:
                    if finished:
                        pe.wait_ge(s.oT_split, 2 * (b - 1))
                    pe.wait_ge(s.k_copied, b + 2)
                    pair_transposes(r[0], m.k_nat, SE).then_inc(s.kT_made, 1)
                if now:
                    transpose_scores(i, u, 2)
                if at_first:
                    pe.wait_ge(s.k_copied, 2)
                    keys_behind_wq(1, 1)
                    pe.wait_ge(s.setup_copied, 3)
                if isinstance(i, int) and b == 1:
                    pe.wait_ge(s.setup_copied, 8)
                if ahead:
                    if at_start:
                        pe.wait_ge(s.wv_split, 2)
                    split_chain(r[3][0:SE, 0:H], lambda k: m.c_h[:, nxt, k, 0:SE], lambda k: m.c_l[:, nxt, k, 0:SE],
                                m.wv_h, m.wv_l, NK).then_inc(s.v_made, 1)
                if before:
                    pe.wait_ge(s.aT_copied, b)
                    chain(r[1][:, 0:HT], lambda k: m.aT[:, k, :],
                          lambda k: m.g[:, k, bass.ds(b - 1, 1), :].rearrange("p b n -> p (b n)"), NX
                          ).then_inc(s.s3_made, 1)
                if alone:
                    put_out(r[3])
                if at_first:
                    pe.wait_ge(s.q_copied, 2)
                    pe.wait_ge(s.m_res_made, 2)
                    keys_behind_wq(2, 2)
                if now:
                    apply_probs(i, u, 1)
                    transpose_scores(i, u, 3)
                if at_start:
                    last_rows_values()
                if ahead:
                    pe.wait_ge(s.q_copied, b + 2)
                    pe.wait_ge(s.m_placed, b + 2)
                    pe.wait_ge(s.kT_copied, b + 2)
                    pair_transposes(r[0], m.q_nat, 128).then_inc(s.qT_made, 1)
                if at_start:
                    last_rows_keys()
                if finished and not alone:
                    put_out(r[2])
                if before:
                    pe.wait_ge(s.p3n_made, b)
                    nc.tensor.transpose(r[1][0:NP3, 0:128], m.p3n[:, :], m.ident[:, :]).then_inc(s.p3T_made, 1)
                if now:
                    apply_probs(i, u, 2)
                if at_first:
                    pe.wait_ge(s.setup_copied, 4)
                    keys_behind_wq(3, 1)
                if ahead:
                    scores(i, u + 1, 0)
                    scores(i, u + 1, 1)
                if before:
                    pe.wait_ge(s.p3T_split, b)
                    if isinstance(i, int) and b == 1:
                        pe.wait_ge(s.v2_placed, 16 * len(V2_PARTS) * HEADS)
                    if not alone:
                        wait(pe, s.y_added, b - 1)
                    mm(r[2][:, 0:H], m.p3T[:, :], m.v2blk[:, bass.ds(b - 1, 1), :].rearrange("p b n -> p (b n)"),
                       start=True, stop=True).then_inc(s.o3_made, 1)
                if at_first:
                    pe.wait_ge(s.setup_copied, 5)
                    keys_behind_wq(4, 2)

            pe.wait_ge(s.ident_made, 1)
            pe.wait_ge(s.k_zeroed, 1)
            pe.wait_ge(s.parts_ones, 6)
            pe.wait_ge(s.w_zeroed, 4)
            run_batches(pe, step)

        @block.scalar
        def _(act):
            act.dma_start(m.wk[:, :, :], wk).then_inc(s.wk_loaded, 16)
            act.dma_start(m.wq[:, :, :], wq).then_inc(s.wq_loaded, 16)

            def copy(dst, src, sem, scale=1.0):
                nc.scalar.activation(dst, src, ACT.Copy, scale=scale).then_inc(sem, 1)

            def by_blocks(bank, rows, n, width=128):
                return bank[0:rows, 0:n * width].rearrange("p (k q) -> p k q", k=n)

            def exps(i, u, unit):
                at = UNITS * (2 * i + u) + unit
                n = SE if unit < 2 else S
                act.wait_ge(s.st_made, at + 1)
                wait(act, s.p_split, at - 1)
                nc.scalar.activation(m.p[0:n, unit % 2, :, :], by_blocks(m.st_bank, n, NC), ACT.Exp
                                     ).then_inc(s.exped, 1)
                wait(act, s.pv_made, at - 1)
                nc.scalar.activation(m.p_hi[0:n, unit % 2, :, :], by_blocks(m.st_bank, n, NC), ACT.Exp
                                     ).then_inc(s.p_hi_made, 1)

            def copy_values():
                act.wait_ge(s.setup_made, 1)
                copy(m.v2_h[:, :], m.ring[1][:, 0:H], s.setup_copied)

            def copy_keys():
                act.wait_ge(s.setup_made, 2)
                copy(m.k2T[:, :, :], by_blocks(m.ring[2], 128, NC), s.setup_copied)

            def copy_keys_behind_wq(n, ring):
                act.wait_ge(s.setup_made, n + 3)
                dst = m.g[:, n // 2, :, :].rearrange("p b (c j t) -> p c b j t", c=NC, j=2)[:, :, :, n % 2, :]
                src = m.ring[ring][0:XR, :].rearrange("p (c b t) -> p c b t", c=NC, b=B)
                copy(dst, src, s.setup_copied, scale=SCALE)

            def first_parts(i, u):
                b, k = 2 * i + u, u % 2
                wait(act, s.v_made, b - 1)
                act.wait_ge(cT_loaded[k], 16 * nth(i, u))
                copy(m.c_h[:, k, :, :], m.cT[:, k, :, :], s.cT_hi_made)
                act.wait_ge(xT_loaded[k], 16 * nth(i, u))
                copy(m.x_h[:, k, :, :], m.xT[:, k, :, :], s.xT_hi_made)

            act.wait_ge(cT_loaded[0], 16)
            copy(m.c_h[:, 0, :, :], m.cT[:, 0, :, :], s.cT_hi_made)
            act.wait_ge(s.wk_loaded, 16)
            copy(m.wk_h[:, :, :], m.wk[:, :, :], s.wk_rounded)
            act.wait_ge(xT_loaded[0], 16)
            copy(m.x_h[:, 0, :, :], m.xT[:, 0, :, :], s.xT_hi_made)
            act.wait_ge(s.wq_loaded, 16)
            copy(m.wq_h[:, :, :], m.wq[:, :, :], s.wq_rounded, scale=SCALE)
            act.wait_ge(s.wv_loaded, 16)
            copy(m.wv_h[:, :, :], m.wv[:, :, :], s.wv_rounded)

            def step(i, u):
                b, nxt, r = 2 * i + u, (u + 1) % 2, m.ring
                now, ahead = live(i, u), live(i, u + 1)
                before, finished = live(i, u - 1), live(i, u - 2)
                at_start = isinstance(i, int) and b == -1
                at_first = isinstance(i, int) and b == 0
                if live(i, u + 2):
                    first_parts(i, u + 2)
                if ahead:
                    act.wait_ge(s.k_made, b + 2)
                    copy(m.k_nat[:, :, 0:D], by_head(r[1][0:SE, 0:H]), s.k_copied)
                if isinstance(i, int) and b == 1:
                    copy_keys_behind_wq(4, 2)
                if finished:
                    act.wait_ge(s.o_summed, b - 1)
                    copy(m.osum[:, H:NX * 128], m.osum[:, H - SLOT:H], s.o_doubled)
                if now:
                    exps(i, u, 0)
                if finished:
                    act.wait_ge(s.oT_made, b - 1)
                    copy(m.o_h[:, :, :], by_blocks(r[0], 128, NX), s.o_hi_made)
                if isinstance(i, int) and b == 1:
                    copy_keys_behind_wq(5, 3)
                if at_first:
                    copy_keys_behind_wq(0, 3)
                if ahead:
                    act.wait_ge(s.qm_made, b + 2)
                    keys = by_head(r[2][:, H:H + HT]).unsqueeze(2)
                    copy(m.m_parts[:, :, 0:3, :], keys.to_broadcast([128, HEADS, 3, T]), s.m_hi_made)
                    copy(m.q_nat[:, :, 0:D], by_head(r[2][:, 0:H]), s.q_copied)
                if now:
                    exps(i, u, 1)
                if ahead:
                    act.wait_ge(s.m_res_made, b + 2)
                    copy(m.m_parts[:, :, 3:5, :], by_head(m.m_res[:, :]).unsqueeze(2).to_broadcast([128, HEADS, 2, T]),
                         s.m_mid_made)
                if before:
                    act.wait_ge(s.aT_made, b)
                    copy(m.aT[:, :, :], by_blocks(r[1], XR, NX), s.aT_copied)
                if ahead:
                    act.wait_ge(x_loaded[nxt], 16 * nth(i, u + 1))
                    wait(act, s.pv_made, UNITS * b)
                    copy(m.x_hi[:, nxt, :, 0:D], by_head(m.x[:, nxt, :]), s.x_hi_made)
                if at_first:
                    copy_keys_behind_wq(1, 1)
                if now:
                    exps(i, u, 2)
                if ahead:
                    act.wait_ge(s.kT_made, b + 2)
                    copy(m.kT[:, :, :], by_blocks(r[0], 128, NC)[:, :, 0:SE], s.kT_copied)
                    act.wait_ge(s.m_split, b + 2)
                    copy(m.q_nat[:, :, D:SLOT].rearrange("p h (n t) -> p h n t", n=NM), m.m_parts[:, :, :, :],
                         s.m_placed)
                    act.wait_ge(s.v_made, b + 2)
                    copy(m.v_hi[:, nxt, :, 0:D], by_head(r[3][0:SE, 0:H]), s.v_hi_made)
                if before:
                    act.wait_ge(s.sh3_made, b)
                    nc.scalar.activation(m.p3[:, :], m.sh3[:, :], ACT.Exp).then_inc(s.p3_made, 1)
                if at_first:
                    copy_keys_behind_wq(2, 2)
                if now:
                    exps(i, u, 3)
                if at_start:
                    copy_values()
                if ahead:
                    act.wait_ge(s.qT_made, b + 2)
                    copy(m.qT[:, :, :], by_blocks(r[0], 128, NC), s.qT_copied)
                if before:
                    act.wait_ge(s.p3T_made, b)
                    copy(m.p3T[:, :], r[1][0:NP3, 0:128], s.p3T_copied)
                if ahead:
                    wait(act, s.v_res_made, b + 1)
                    copy(m.v_nat[:, :], r[3][0:SE, 0:H], s.v_copied)
                    copy(m.m_st[:, :, :], by_blocks(r[0], 128, NC), s.m_stacked)
                    act.wait_ge(s.v_res_made, b + 2)
                    copy(m.v_mid[:, nxt, :, 0:D], by_head(m.v_res[:, :]), s.v_mid_made)
                    if at_start:
                        copy_keys()
                    if at_first:
                        copy_keys_behind_wq(3, 1)
                if at_start:
                    act.wait_ge(s.wout_loaded, 16)
                    copy(m.wout_h[:, :, :], m.wout[:, :, :], s.wout_rounded)

            run_batches(act, step)

        @block.vector
        def _(dve):
            v = nc.vector
            r = m.ring

            parts = ((m.wk_l, NK), (m.wq_l, NX), (m.wv_l, NK), (m.wout_l, NX))
            for l, n in parts:
                v.memset(l[SLOT:128, n - 1, :].bitcast(mybir.dt.float32), 0.0).then_inc(s.w_zeroed, 1)

            v.memset(m.v2blk[:, 2 * B // 4:3 * B // 4, :].bitcast(mybir.dt.float32), 0.0).then_inc(s.v2_zeroed, 1)

            def split_weights(w, h, l, n, rounded, split, scale=1.0):
                dve.wait_ge(rounded, 1)
                for rows, chunks in ((slice(0, 128), slice(0, n - 1)), (slice(0, SLOT), slice(n - 1, n))):
                    v.scalar_tensor_tensor(l[rows, chunks, :], w[rows, chunks, :], scale, h[rows, chunks, :],
                                           ALU.mult, ALU.subtract).then_inc(split, 1)

            split_weights(m.wk, m.wk_h, m.wk_l, NK, s.wk_rounded, s.wk_split)
            split_weights(m.wq, m.wq_h, m.wq_l, NX, s.wq_rounded, s.wq_split, SCALE)
            split_weights(m.wv, m.wv_h, m.wv_l, NK, s.wv_rounded, s.wv_split)
            v.memset(m.v2blk[:, 3 * B // 4:B, :].bitcast(mybir.dt.float32), 0.0).then_inc(s.v2_zeroed, 1)

            def over(t, n):
                return t.unsqueeze(2).to_broadcast([t.shape[0], t.shape[1], n])

            def unit_scores(unit):
                n = SE if unit < 2 else S
                return n, m.s_bank[unit % 2][:, 0:NC * n].rearrange("p (c k) -> p c k", c=NC)

            def find_max(i, u, unit):
                dve.wait_ge(s.s_made, UNITS * (2 * i + u) + unit + 1)
                v.tensor_reduce(m.smax[:, unit % 2, :], unit_scores(unit)[1], AX.X, ALU.max).then_inc(s.maxed, 1)

            def shift(i, u, unit, maxima):
                (n, src), b = unit_scores(unit), 2 * i + u
                dve.wait_ge(s.maxed, UNITS * b + maxima)
                wait(dve, s.st_made, UNITS * b + unit - 1)
                v.tensor_tensor(m.shift[:, unit % 2, :, 0:n], src, over(m.smax[:, unit % 2, :], n),
                                ALU.subtract).then_inc(s.shifted, 1)

            def split_probs(i, u, unit):
                n, at = (SE if unit < 2 else S), UNITS * (2 * i + u) + unit
                dve.wait_ge(s.p_hi_made, at + 1)
                v.tensor_tensor(m.p_lo[0:n, unit % 2, :, :], m.p[0:n, unit % 2, :, :], m.p_hi[0:n, unit % 2, :, :],
                                ALU.subtract).then_inc(s.p_split, 1)

            products = m.pv_bank[:, 0:NC * (D + 1)].rearrange("p (c d) -> p c d", c=NC)

            def invert_sums(i, u, unit):
                dve.wait_ge(s.pv_made, UNITS * (2 * i + u) + unit + 1)
                v.reciprocal(m.rec[:, unit % 2, :], products[:, :, D]).then_inc(s.reced, 1)

            def normalise(i, u, unit):
                dve.wait_ge(s.reced, UNITS * (2 * i + u) + unit + 1)
                dst = (m.hs[:, u % 2, :] if unit < 2 else m.ca[:, :]).rearrange("p (c j d) -> p c j d", c=NC, j=2)
                v.tensor_tensor(dst[:, :, unit % 2, :], products[:, :, 0:D], over(m.rec[:, unit % 2, :], D), ALU.mult
                                ).then_inc(s.normed, 1)

            def step(i, u):
                b, nxt = 2 * i + u, (u + 1) % 2
                now, ahead = live(i, u), live(i, u + 1)
                before, finished = live(i, u - 1), live(i, u - 2)
                sh3, p3, s3 = (by_head(t) for t in (m.sh3[:, :], m.p3[:, :], r[1][:, 0:HT]))
                copies = len(V2_PARTS)
                p3n = m.p3n[:, :].rearrange("p (n h t) -> p n h t", n=copies, h=HEADS)
                many = [128, copies, HEADS, T]
                alone = before and not now

                def add_residual(bank):
                    dve.wait_ge(s.y_made, b - 1)
                    dve.wait_ge(s.xb_made, b - 1)
                    wait(dve, stored[u % 2], 16 * (nth(i, u - 2) - 1))
                    v.tensor_tensor(m.y[:, u % 2, :], bank[:, 0:H], m.xb[:, u % 2, :], ALU.add
                                    ).then_inc(s.y_added, 1)

                if alone:
                    invert_sums(i, u - 1, 3)
                    normalise(i, u - 1, 3)
                if before and now:
                    invert_sums(i, u - 1, 3)
                if now:
                    find_max(i, u, 2)
                if before and now:
                    normalise(i, u - 1, 3)
                if now:
                    split_probs(i, u, 0)
                if finished:
                    src = r[0][:, 0:NX * 128].rearrange("p (k q) -> p k q", k=NX)
                    dve.wait_ge(s.o_hi_made, b - 1)
                    v.tensor_tensor(m.o_l[:, :, :], src[:, 0:NX - 1, :], m.o_h[:, 0:NX - 1, :], ALU.subtract
                                    ).then_inc(s.oT_split, 1)
                    v.tensor_tensor(m.o_h[SLOT:128, NX - 1, :], src[SLOT:128, NX - 1, :],
                                    m.o_h[SLOT:128, NX - 1, :], ALU.subtract).then_inc(s.oT_split, 1)
                if now:
                    shift(i, u, 2, 3)
                if ahead:
                    dve.wait_ge(s.m_hi_made, b + 2)
                    dve.wait_ge(s.q_copied, b + 2)
                    v.tensor_tensor(by_head(m.m_res[:, :]), by_head(r[2][:, H:H + HT]), m.m_parts[:, :, 0, :],
                                    ALU.subtract).then_inc(s.m_res_made, 1)
                if now:
                    split_probs(i, u, 1)
                    invert_sums(i, u, 0)
                    find_max(i, u, 3)
                    normalise(i, u, 0)
                    shift(i, u, 3, 4)
                if ahead:
                    dve.wait_ge(s.m_mid_made, b + 2)
                    v.tensor_tensor(m.m_parts[:, :, 5, :], by_head(m.m_res[:, :]), m.m_parts[:, :, 3, :],
                                    ALU.subtract).then_inc(s.m_split, 1)
                if before:
                    dve.wait_ge(s.s3_made, b)
                    v.tensor_reduce(m.max3[:, :], s3, AX.X, ALU.max).then_inc(s.max3_made, 1)
                if isinstance(i, int) and b == -1:
                    dve.wait_ge(s.setup_copied, 1)
                    v.tensor_tensor(m.v2_l[:, :], r[1][:, 0:H], m.v2_h[:, :], ALU.subtract).then_inc(s.v2_split, 1)
                if isinstance(i, int) and b == 0:
                    split_weights(m.wout, m.wout_h, m.wout_l, NX, s.wout_rounded, s.wout_split)
                if before:
                    dve.wait_ge(s.max3_made, b)
                    v.tensor_tensor(sh3, s3, over(m.max3[:, :], T), ALU.subtract).then_inc(s.sh3_made, 1)
                if now:
                    split_probs(i, u, 2)
                    invert_sums(i, u, 1)
                if before:
                    dve.wait_ge(s.p3_made, b)
                    v.tensor_reduce(m.sum3[:, :], p3, AX.X, ALU.add).then_inc(s.sum3_made, 1)
                if now:
                    normalise(i, u, 1)
                if before:
                    dve.wait_ge(s.sum3_made, b)
                    v.reciprocal(m.rec3[:, :], m.sum3[:, :]).then_inc(s.rec3_made, 1)
                    dve.wait_ge(s.rec3_made, b)
                    v.tensor_tensor(p3n, p3.unsqueeze(1).to_broadcast(many),
                                    m.rec3[:, :].unsqueeze(1).unsqueeze(3).to_broadcast(many), ALU.mult
                                    ).then_inc(s.p3n_made, 1)
                if now:
                    split_probs(i, u, 3)
                if finished and not alone:
                    add_residual(r[2])
                if before:
                    dve.wait_ge(s.p3T_copied, b)
                    v.tensor_tensor(m.p3T[HT:2 * HT, :], r[1][HT:2 * HT, 0:128], m.p3T[HT:2 * HT, :],
                                    ALU.subtract).then_inc(s.p3T_split, 1)
                if now:
                    invert_sums(i, u, 2)
                    normalise(i, u, 2)
                if ahead:
                    find_max(i, u + 1, 0)
                    shift(i, u + 1, 0, 1)
                    find_max(i, u + 1, 1)
                if before:
                    dve.wait_ge(s.o3_made, b)
                    v.tensor_tensor(m.osum[:, 0:H], r[2][:, 0:H], m.hs[:, (u - 1) % 2, :], ALU.add
                                    ).then_inc(s.o_summed, 1)
                if ahead:
                    shift(i, u + 1, 1, 2)
                if alone:
                    add_residual(r[3])

            run_batches(dve, step)


def kernel(x, ctx_768, L0_xattn_Wq, L0_xattn_Wk, L0_xattn_Wv, L0_xattn_Wq_ca, L0_xattn_Wk_ca, L0_xattn_Wv_ca,
           L0_xattn_Wout, L0_xattn_b_out):
    import numpy as np
    import concourse.bacc as bacc
    from concourse.bass_utils import run_bass_kernel_spmd

    f = np.float32
    x, c, wq, wk, wv, wq_ca, wk_ca, wv_ca, wout, bias = (np.asarray(a) for a in (
        x, ctx_768, L0_xattn_Wq, L0_xattn_Wk, L0_xattn_Wv, L0_xattn_Wq_ca, L0_xattn_Wk_ca, L0_xattn_Wv_ca,
        L0_xattn_Wout, L0_xattn_b_out))

    def by_threes(w):
        out = np.zeros((XR, NX) + w.shape[1:], f)
        out[:, 0], out[:, 1], out[D:, 2] = w[0:XR], w[XR:2 * XR], w[2 * XR:]
        return out

    def by_rows(w):
        n = -(-len(w) // 128)
        out = np.empty((128, n) + w.shape[1:], f)
        for k in range(n - 1):
            out[:, k] = w[k * 128:(k + 1) * 128]
        out[0:SLOT, n - 1] = out[SLOT:128, n - 1] = w[(n - 1) * 128:]
        return out

    def by_halves(w):
        return w.reshape(NK, CR, -1).transpose(1, 0, 2)

    wq_and_ca = np.zeros((H, H + HT), f)
    wq_and_ca[:, 0:H] = wq
    wkca_pad = np.zeros((CR, NK, NC, 2, SLOT), f)
    wkca_pad[..., 0:D] = by_halves(wk_ca).reshape(CR, NK, NC, 2, D)
    wqT = np.zeros((2, SLOT, NX, NC, XR), f)
    wqT[:, 0:D] = by_threes(wq).reshape(XR, NX, NC, 2, D).transpose(3, 4, 1, 2, 0)
    signs = np.zeros((2, SLOT, 2), f)
    for h in range(HEADS):
        wq_and_ca[h * D:(h + 1) * D, H + h * T:H + (h + 1) * T] = wq_ca[:, h * D:(h + 1) * D].T
    for n, part in enumerate(QUERY_PARTS):
        signs[:, D + T * n:D + T * (n + 1), 0] = -1.0 if part >= 1 else 0.0
        signs[:, D + T * n:D + T * (n + 1), 1] = -1.0 if part == 2 else 0.0

    xT = np.stack([by_rows(a.T) for a in x])
    cT = np.stack([by_rows(a.T) for a in c])
    at = np.linspace(0, CAD - 1, S).astype(np.int64)
    c_rows = np.tile(c[:, SE:, at], (1, NM, 1))
    caT = by_halves(c[:, SE:, :].reshape(B * T, CAD).T)

    arrays = {
        "x": x, "xT": xT, "cT": cT, "c_rows": c_rows, "caT": caT, "wq": by_rows(wq_and_ca),
        "wk": by_rows(wk), "wv": by_rows(wv), "wkca": wkca_pad.reshape(CR, NK, NC, 128),
        "wvca": by_halves(wv_ca), "wqT": wqT.reshape(128, NX, NC, XR), "wout": by_rows(wout),
        "bias": np.broadcast_to(bias, (128, H)), "signs": signs.reshape(128, 2),
    }
    arrays = {f"in_{k}": np.ascontiguousarray(a) for k, a in arrays.items()}
    nc = bacc.Bacc("TRN2", target_bir_lowering=False, num_devices=1)
    args = [nc.dram_tensor(k, a.shape, mybir.dt.float32, kind="ExternalInput").ap() for k, a in arrays.items()]
    out = nc.dram_tensor("out", (B, S, H), mybir.dt.float32, kind="ExternalOutput").ap()
    v2_parts = nc.dram_tensor("v2_parts", (2, B * T, H), mybir.dt.float32).ap()
    xattn_kernel(nc, *args, out, v2_parts)
    return run_bass_kernel_spmd(nc, [arrays], core_ids=[0]).results[0]["out"]
```
